# Optimizing a Trainium2 kernel written in Bass

```python
import numpy as np
import jax
import jax.numpy as jnp

def _softmax(x, axis=-1):
    return jax.nn.softmax(x, axis=axis)

def _gelu(x):
    return jax.nn.gelu(x, approximate=True)

def _silu(x):
    return jax.nn.silu(x)

def _sigmoid(x):
    return jax.nn.sigmoid(x)

def _layernorm(x, axis=-1, eps=1e-05):
    m = jnp.mean(x, axis=axis, keepdims=True)
    v = jnp.var(x, axis=axis, keepdims=True)
    return (x - m) / jnp.sqrt(v + eps)

def _scatter_add(tgt, idx, src, axis=0):
    return tgt.at[idx].add(src)

def _segment_sum(src, seg, n):
    return jax.ops.segment_sum(src, seg, n)
kernel_name = 'mk_flamingo_gated_d2_seqx_r8_46d15c'

def setup_inputs(seed: int=0):
    np.random.seed(seed)
    _w = jnp.asarray

    def _rec_inputs():
        import jax
        import jax.numpy as jnp
        _rk = jax.random.key(seed)
        x = 7.22e-05 + 1 * jax.random.normal(jax.random.fold_in(_rk, 1), (2, 256, 128), jnp.float32)
        _lenS = 256 - jax.random.randint(jax.random.fold_in(_rk, 7), (2,), 0, max(1, 256 // 4) + 1, jnp.int32)
        _lenS2 = 512 - jax.random.randint(jax.random.fold_in(_rk, 8), (2,), 0, max(1, 512 // 4) + 1, jnp.int32)
        _ctx_1024P = jax.random.normal(jax.random.fold_in(_rk, 11), (2, 16, 128), jnp.float32)
        _ctx_1024c = jax.random.dirichlet(jax.random.fold_in(_rk, 511), 0.3 * jnp.ones((16,), jnp.float32), (2, 512))
        _ctx_1024t = jnp.einsum('bsk,bkd->bsd', _ctx_1024c, _ctx_1024P)
        _ctx_1024t = _ctx_1024t * jax.lax.rsqrt(jnp.mean(jnp.square(_ctx_1024t)) + 1e-12) * 0.953939
        ctx_1024 = 4.13588e-05 + 0.999923 * (_ctx_1024t + 0.3 * jax.random.normal(jax.random.fold_in(_rk, 611), (2, 512, 128), jnp.float32))
        _validS = jnp.arange(256)[None, :] < _lenS[:, None]
        _validS2 = jnp.arange(512)[None, :] < _lenS2[:, None]
        _causal = jnp.tril(jnp.ones((256, 256), dtype=bool))
        mask_1x1xSxS2_bk0 = jnp.logical_not(jnp.broadcast_to(_validS2[0:1, None, None, :], (1, 1, 256, 512)))
        mask_BxSxS2_bk1 = jnp.broadcast_to(_validS2[:, None, :], (2, 256, 512))
        _g = jax.random.normal(jax.random.fold_in(_rk, 9001), (2, 2), jnp.float32)
        _g = jnp.sign(_g) * jnp.maximum(jnp.abs(_g), 1.0) + (_g == 0) * 1.0
        g_xattn = _g[0]
        g_ffn = _g[1]
        return (x, ctx_1024, mask_1x1xSxS2_bk0, mask_BxSxS2_bk1, g_xattn, g_ffn)
    x, ctx_1024, mask_1x1xSxS2_bk0, mask_BxSxS2_bk1, g_xattn, g_ffn = _rec_inputs()

    def _L0_xattn_setup():
        import jax, jax.numpy as jnp
        import numpy as np
        import math
        EMBED_DIM = 128
        NUM_HEADS = 16
        HEAD_DIM = EMBED_DIM // NUM_HEADS
        B, S = (4, 256)
        key = jax.random.key(seed)
        ks = jax.random.split(key, 7)
        std = math.sqrt(2.0 / EMBED_DIM)
        inp = {'query': jax.random.normal(ks[0], (B, S, EMBED_DIM), dtype=jnp.float32), 'key': jax.random.normal(ks[1], (B, S, EMBED_DIM), dtype=jnp.float32), 'value': jax.random.normal(ks[2], (B, S, EMBED_DIM), dtype=jnp.float32), 'Wq': jax.random.normal(ks[3], (EMBED_DIM, EMBED_DIM), dtype=jnp.float32) * std, 'bq': jnp.zeros((EMBED_DIM,), dtype=jnp.float32), 'Wk': jax.random.normal(ks[4], (EMBED_DIM, EMBED_DIM), dtype=jnp.float32) * std, 'bk': jnp.zeros((EMBED_DIM,), dtype=jnp.float32), 'Wv': jax.random.normal(ks[5], (EMBED_DIM, EMBED_DIM), dtype=jnp.float32) * std, 'bv': jnp.zeros((EMBED_DIM,), dtype=jnp.float32), 'Wo': jax.random.normal(ks[6], (EMBED_DIM, EMBED_DIM), dtype=jnp.float32) * std, 'bo': jnp.zeros((EMBED_DIM,), dtype=jnp.float32), 'mask': jnp.tril(jnp.ones((S, S), dtype=bool))[None, None, :, :]}
        return inp
    _L0_xattn_all = _L0_xattn_setup()
    _L0_xattn_in = {k: v for k, v in _L0_xattn_all.items() if k in ('Wq', 'bq', 'Wk', 'bk', 'Wv', 'bv', 'Wo', 'bo')}
    del _L0_xattn_all

    def _L0_ffn_setup():
        import jax, jax.numpy as jnp
        import numpy as np
        IN_FEATURES = 128
        ACT_BITS = 4

        def _hadamard(size: int) -> np.ndarray:
            h = np.array([[1.0]], dtype=np.float64)
            while h.shape[0] < size:
                h = np.block([[h, h], [h, -h]])
            return (h / np.sqrt(size)).astype(np.float32)

        def _quantize_activations(x, bits=ACT_BITS):
            pos = 2 ** (bits - 1) - 1
            neg = 2 ** (bits - 1)
            scale = jnp.clip(jnp.max(jnp.abs(jax.lax.stop_gradient(x)), axis=-1, keepdims=True), 1e-05) / pos
            q = jnp.clip(jnp.round(x / scale), -neg, pos) * scale
            return x + jax.lax.stop_gradient(q - x)

        def _ternary_quantize_ste(w):
            scale = jnp.clip(jnp.mean(jnp.abs(jax.lax.stop_gradient(w)), axis=1, keepdims=True), 1e-05)
            n = w / scale
            tern = jnp.where(n > 0.5, 1.0, jnp.where(n < -0.5, -1.0, 0.0))
            q = tern * scale
            return w + jax.lax.stop_gradient(q - w)
        key = jax.random.key(seed)
        k1, k2 = jax.random.split(key)
        x = jax.random.normal(k1, (8, 1024, IN_FEATURES), dtype=jnp.float32)
        bound = 1.0 / np.sqrt(IN_FEATURES)
        weight = jax.random.uniform(k2, (128, IN_FEATURES), dtype=jnp.float32, minval=-bound, maxval=bound)
        return {'x': x, 'weight': weight}
    _L0_ffn_all = _L0_ffn_setup()
    _L0_ffn_in = {k: v for k, v in _L0_ffn_all.items() if k in ('weight',)}
    del _L0_ffn_all

    def _L1_xattn_setup():
        import jax, jax.numpy as jnp
        import numpy as np
        D_MODEL = 128
        NUM_HEADS = 16
        D_K = 64
        D_V = 64
        B, L = (2, 256)
        key = jax.random.key(seed)
        ks = jax.random.split(key, 12)
        std_qk = np.sqrt(2.0 / (D_MODEL + D_K)).astype(np.float32)
        std_v = np.sqrt(2.0 / (D_MODEL + D_V)).astype(np.float32)
        return {'input_Q': jax.random.normal(ks[0], (B, L, D_MODEL), jnp.float32), 'input_K': jax.random.normal(ks[1], (B, L, D_MODEL), jnp.float32), 'input_V': jax.random.normal(ks[2], (B, L, D_MODEL), jnp.float32), 'attn_mask': jax.random.randint(ks[3], (B, L, L), 0, 2).astype(jnp.bool_), 'W_Q': std_qk * jax.random.normal(ks[4], (NUM_HEADS * D_K, D_MODEL), jnp.float32), 'b_Q': jnp.zeros((NUM_HEADS * D_K,), jnp.float32), 'W_K': std_qk * jax.random.normal(ks[5], (NUM_HEADS * D_K, D_MODEL), jnp.float32), 'b_K': jnp.zeros((NUM_HEADS * D_K,), jnp.float32), 'W_V': std_v * jax.random.normal(ks[6], (NUM_HEADS * D_V, D_MODEL), jnp.float32), 'b_V': jnp.zeros((NUM_HEADS * D_V,), jnp.float32), 'W_out': std_v * jax.random.normal(ks[7], (D_MODEL, NUM_HEADS * D_V), jnp.float32), 'b_out': jnp.zeros((D_MODEL,), jnp.float32)}
    _L1_xattn_all = _L1_xattn_setup()
    _L1_xattn_in = {k: v for k, v in _L1_xattn_all.items() if k in ('W_Q', 'b_Q', 'W_K', 'b_K', 'W_V', 'b_V', 'W_out', 'b_out')}
    del _L1_xattn_all

    def _L1_ffn_setup():
        import jax, jax.numpy as jnp
        import numpy as np
        TOP_K = 4
        CAP_FACTOR = 4

        def swiglu(x, w1, w2, w3):
            return jax.nn.silu(x @ w1) * (x @ w3) @ w2
        key = jax.random.key(seed)
        ks = jax.random.split(key, 8)
        B, S, D, H, E = (2, 256, 128, 64, 32)
        Hs = 2 * H
        sd = lambda *sh: 1.0 / np.sqrt(sh[-2])
        x = jax.random.normal(ks[0], (B, S, D), dtype=jnp.float32)
        Wg = jax.random.normal(ks[1], (D, E), dtype=jnp.float32) * (1.0 / np.sqrt(D))
        W1 = jax.random.normal(ks[2], (E, D, H), dtype=jnp.float32) * (1.0 / np.sqrt(D))
        W3 = jax.random.normal(ks[3], (E, D, H), dtype=jnp.float32) * (1.0 / np.sqrt(D))
        W2 = jax.random.normal(ks[4], (E, H, D), dtype=jnp.float32) * (1.0 / np.sqrt(H))
        Ws1 = jax.random.normal(ks[5], (D, Hs), dtype=jnp.float32) * (1.0 / np.sqrt(D))
        Ws3 = jax.random.normal(ks[6], (D, Hs), dtype=jnp.float32) * (1.0 / np.sqrt(D))
        Ws2 = jax.random.normal(ks[7], (Hs, D), dtype=jnp.float32) * (1.0 / np.sqrt(Hs))
        return {'x': x, 'Wg': Wg, 'W1': W1, 'W2': W2, 'W3': W3, 'Ws1': Ws1, 'Ws2': Ws2, 'Ws3': Ws3}
    _L1_ffn_all = _L1_ffn_setup()
    _L1_ffn_in = {k: v for k, v in _L1_ffn_all.items() if k in ('Wg', 'W1', 'W2', 'W3', 'Ws1', 'Ws2', 'Ws3')}
    del _L1_ffn_all
    return {'x': x, 'ctx_1024': ctx_1024, 'mask_1x1xSxS2_bk0': mask_1x1xSxS2_bk0, 'mask_BxSxS2_bk1': mask_BxSxS2_bk1, 'g_xattn': g_xattn, 'g_ffn': g_ffn, 'L0_xattn_Wq': _L0_xattn_in['Wq'], 'L0_xattn_bq': _L0_xattn_in['bq'], 'L0_xattn_Wk': _L0_xattn_in['Wk'], 'L0_xattn_bk': _L0_xattn_in['bk'], 'L0_xattn_Wv': _L0_xattn_in['Wv'], 'L0_xattn_bv': _L0_xattn_in['bv'], 'L0_xattn_Wo': _L0_xattn_in['Wo'], 'L0_xattn_bo': _L0_xattn_in['bo'], 'L0_ffn_weight': _L0_ffn_in['weight'], 'L1_xattn_W_Q': _L1_xattn_in['W_Q'], 'L1_xattn_b_Q': _L1_xattn_in['b_Q'], 'L1_xattn_W_K': _L1_xattn_in['W_K'], 'L1_xattn_b_K': _L1_xattn_in['b_K'], 'L1_xattn_W_V': _L1_xattn_in['W_V'], 'L1_xattn_b_V': _L1_xattn_in['b_V'], 'L1_xattn_W_out': _L1_xattn_in['W_out'], 'L1_xattn_b_out': _L1_xattn_in['b_out'], 'L1_ffn_Wg': _L1_ffn_in['Wg'], 'L1_ffn_W1': _L1_ffn_in['W1'], 'L1_ffn_W2': _L1_ffn_in['W2'], 'L1_ffn_W3': _L1_ffn_in['W3'], 'L1_ffn_Ws1': _L1_ffn_in['Ws1'], 'L1_ffn_Ws2': _L1_ffn_in['Ws2'], 'L1_ffn_Ws3': _L1_ffn_in['Ws3']}

def reference(x, ctx_1024, mask_1x1xSxS2_bk0, mask_BxSxS2_bk1, g_xattn, g_ffn, L0_xattn_Wq, L0_xattn_bq, L0_xattn_Wk, L0_xattn_bk, L0_xattn_Wv, L0_xattn_bv, L0_xattn_Wo, L0_xattn_bo, L0_ffn_weight, L1_xattn_W_Q, L1_xattn_b_Q, L1_xattn_W_K, L1_xattn_b_K, L1_xattn_W_V, L1_xattn_b_V, L1_xattn_W_out, L1_xattn_b_out, L1_ffn_Wg, L1_ffn_W1, L1_ffn_W2, L1_ffn_W3, L1_ffn_Ws1, L1_ffn_Ws2, L1_ffn_Ws3):
    import jax
    import jax.numpy as jnp

    def _L0_xattn_ref(query, key, value, Wq, bq, Wk, bk, Wv, bv, Wo, bo, mask):
        import jax, jax.numpy as jnp
        import numpy as np
        import math
        EMBED_DIM = 128
        NUM_HEADS = 16
        HEAD_DIM = EMBED_DIM // NUM_HEADS
        B, S = (4, 256)
        Bt, St, E = query.shape
        H, D = (NUM_HEADS, HEAD_DIM)
        q = (query @ Wq.T + bq).reshape(Bt, St, H, D).transpose(0, 2, 1, 3)
        k = (key @ Wk.T + bk).reshape(Bt, -1, H, D).transpose(0, 2, 1, 3)
        v = (value @ Wv.T + bv).reshape(Bt, -1, H, D).transpose(0, 2, 1, 3)
        scores = jnp.einsum('bhqd,bhkd->bhqk', q, k) / math.sqrt(D)
        neg_inf = jnp.asarray(jnp.finfo(scores.dtype).min, scores.dtype)
        scores = jnp.where(mask, scores, neg_inf)
        attention = jax.nn.softmax(scores, axis=-1)
        out = jnp.einsum('bhqk,bhkd->bhqd', attention, v)
        out = out.transpose(0, 2, 1, 3).reshape(Bt, St, E)
        return out @ Wo.T + bo

    def _L0_ffn_ref(x, weight):
        import jax, jax.numpy as jnp
        import numpy as np
        IN_FEATURES = 128
        ACT_BITS = 4

        def _hadamard(size: int) -> np.ndarray:
            h = np.array([[1.0]], dtype=np.float64)
            while h.shape[0] < size:
                h = np.block([[h, h], [h, -h]])
            return (h / np.sqrt(size)).astype(np.float32)

        def _quantize_activations(x, bits=ACT_BITS):
            pos = 2 ** (bits - 1) - 1
            neg = 2 ** (bits - 1)
            scale = jnp.clip(jnp.max(jnp.abs(jax.lax.stop_gradient(x)), axis=-1, keepdims=True), 1e-05) / pos
            q = jnp.clip(jnp.round(x / scale), -neg, pos) * scale
            return x + jax.lax.stop_gradient(q - x)

        def _ternary_quantize_ste(w):
            scale = jnp.clip(jnp.mean(jnp.abs(jax.lax.stop_gradient(w)), axis=1, keepdims=True), 1e-05)
            n = w / scale
            tern = jnp.where(n > 0.5, 1.0, jnp.where(n < -0.5, -1.0, 0.0))
            q = tern * scale
            return w + jax.lax.stop_gradient(q - w)
        H = jnp.asarray(_hadamard(IN_FEATURES))
        xh = x @ H
        xq = _quantize_activations(xh)
        wq = _ternary_quantize_ste(weight)
        return jnp.einsum('bsi,oi->bso', xq, wq)

    def _L1_xattn_ref(input_Q, input_K, input_V, attn_mask, W_Q, b_Q, W_K, b_K, W_V, b_V, W_out, b_out):
        import jax, jax.numpy as jnp
        import numpy as np
        D_MODEL = 128
        NUM_HEADS = 16
        D_K = 64
        D_V = 64
        B, L = (2, 256)
        batch = input_Q.shape[0]
        Q = (input_Q @ W_Q.T + b_Q).reshape(batch, -1, NUM_HEADS, D_K).transpose(0, 2, 1, 3)
        K = (input_K @ W_K.T + b_K).reshape(batch, -1, NUM_HEADS, D_K).transpose(0, 2, 1, 3)
        V = (input_V @ W_V.T + b_V).reshape(batch, -1, NUM_HEADS, D_V).transpose(0, 2, 1, 3)
        scores = jnp.einsum('bhqd,bhkd->bhqk', Q, K) / np.sqrt(D_K).astype(np.float32)
        scores = jnp.where(attn_mask[:, None, :, :], jnp.float32(-10000.0), scores)
        attn = jax.nn.softmax(scores, axis=-1)
        out = jnp.einsum('bhqk,bhkd->bhqd', attn, V)
        out = out.transpose(0, 2, 1, 3).reshape(batch, -1, NUM_HEADS * D_V)
        return out @ W_out.T + b_out

    def _L1_ffn_ref(x, Wg, W1, W2, W3, Ws1, Ws2, Ws3):
        import jax, jax.numpy as jnp
        import numpy as np
        TOP_K = 4
        CAP_FACTOR = 4

        def swiglu(x, w1, w2, w3):
            return jax.nn.silu(x @ w1) * (x @ w3) @ w2
        B, S, D = x.shape
        E = Wg.shape[1]
        T = B * S
        xf = x.reshape(T, D)
        scores = jax.nn.softmax(xf @ Wg, axis=-1)
        weights, indices = jax.lax.top_k(scores, TOP_K)
        P = T * TOP_K
        pair_expert = indices.reshape(-1)
        pair_token = jnp.repeat(jnp.arange(T), TOP_K)
        pair_weight = weights.reshape(-1).astype(xf.dtype)
        C = CAP_FACTOR * P // E
        y = jnp.zeros_like(xf)
        for e in range(E):
            pos = jnp.nonzero(pair_expert == e, size=C, fill_value=P)[0]
            valid = pos < P
            safe = jnp.minimum(pos, P - 1)
            tok = jnp.where(valid, pair_token[safe], 0)
            w = jnp.where(valid, pair_weight[safe], 0.0)
            xg = xf[tok]
            out = swiglu(xg, W1[e], W2[e], W3[e]) * w[:, None]
            y = y.at[tok].add(out)
        z = swiglu(xf, Ws1, Ws2, Ws3)
        return (y + z).reshape(B, S, D)
    x = x + jnp.tanh(g_xattn[0]) * _L0_xattn_ref(_layernorm(x, axis=-1), ctx_1024, ctx_1024, L0_xattn_Wq, L0_xattn_bq, L0_xattn_Wk, L0_xattn_bk, L0_xattn_Wv, L0_xattn_bv, L0_xattn_Wo, L0_xattn_bo, mask_1x1xSxS2_bk0)
    x = x + jnp.tanh(g_ffn[0]) * _L0_ffn_ref(_layernorm(x, axis=-1), L0_ffn_weight)
    x = x + jnp.tanh(g_xattn[1]) * _L1_xattn_ref(_layernorm(x, axis=-1), ctx_1024, ctx_1024, mask_BxSxS2_bk1, L1_xattn_W_Q, L1_xattn_b_Q, L1_xattn_W_K, L1_xattn_b_K, L1_xattn_W_V, L1_xattn_b_V, L1_xattn_W_out, L1_xattn_b_out)
    x = x + jnp.tanh(g_ffn[1]) * _L1_ffn_ref(_layernorm(x, axis=-1), L1_ffn_Wg, L1_ffn_W1, L1_ffn_W2, L1_ffn_W3, L1_ffn_Ws1, L1_ffn_Ws2, L1_ffn_Ws3)
    return x

_drawn_inputs = setup_inputs


def setup_inputs(seed=0):
    import zlib

    import numpy as np

    out = dict(_drawn_inputs(seed))
    spreads = {'g_ffn': (-1.0, 0.6),
     'L0_xattn_bq': (0.0, 0.1),
     'L0_xattn_bk': (0.0, 0.8),
     'L0_xattn_bv': (0.0, 0.1),
     'L0_xattn_bo': (0.0, 0.1),
     'L1_xattn_b_Q': (0.0, 0.1),
     'L1_xattn_b_K': (0.0, 0.8),
     'L1_xattn_b_V': (0.0, 0.1),
     'L1_xattn_b_out': (0.0, 0.1)}
    factors = {}
    for name, (base, spread) in spreads.items():
        noise = np.random.default_rng([zlib.crc32(name.encode()), seed]).standard_normal(out[name].shape)
        drawn = base * np.exp(spread * noise) if base else spread * noise
        out[name] = jnp.asarray(drawn.astype(out[name].dtype))
    for name, factor in factors.items():
        out[name] = (out[name] * factor).astype(out[name].dtype)
    return out
```

```python
import concourse.bass as bass
from concourse import mybir
from contextlib import ExitStack

F32 = mybir.dt.float32
F32R = mybir.dt.float32r
BF16 = mybir.dt.bfloat16
U8 = mybir.dt.uint8
ALU = mybir.AluOpType
ACT = mybir.ActivationFunctionType
X = mybir.AxisListType.X

P = 128
B, SQ, SK = 2, 256, 512
TOK = B * SQ
NT = TOK // P
NC = B * SK // P
NQ = SQ // P
NK = SK // P
HEADS = 16
LN_EPS = 1e-5
FAR = 1.7e38
EXPERTS, HID, TOP = 32, 64, 4
CAP = 4 * TOK * TOP // EXPERTS
PAIRS = EXPERTS // 2
JOBS = ("weights", "k0", "q", "k1", "v0", "v1")


def build(nc, a, out):
    ctx = ExitStack()
    with ctx:
        def sb(name, shape, dt=F32):
            return ctx.enter_context(nc.sbuf_tensor(name, shape, dt))

        def sem(name):
            return ctx.enter_context(nc.semaphore(name))

        bank = [ctx.enter_context(nc.psum_tensor(f"bank{i}", [P, 512], F32)) for i in range(8)]
        score_bank = bank[0:3]
        turn_bank = bank[3:5]
        mix_bank, job_bank, y_bank = bank[5], bank[6], bank[7]

        ident = sb("ident", [P, P])
        had = sb("had", [P, P])
        lo_k = sb("lo_k", [P, 1])
        lo_q = sb("lo_q", [P, 1])
        head_row = sb("head_row", [P, 4])
        gates = sb("gates", [P, 4])
        tanh_g = sb("tanh_g", [P, 4])
        x_sb = sb("x_sb", [P, NT, P])
        ctx_sb = sb("ctx_sb", [P, NC, P])
        ctxT = sb("ctxT", [P, NC * P])
        xn = sb("xn", [P, NT, P])
        xnT = sb("xnT", [P, TOK])
        stats = sb("stats", [P, NT, 6])
        mv = sb("mv", [P, NT, 2])
        veps = sb("veps", [P, NT])
        neg_half = sb("neg_half", [P, NT])
        rstd = sb("rstd", [P, NT])
        tmp = sb("tmp", [P, NT, P])

        NS, NP, NCOL = 3, 6, 8
        masked = sb("masked", [P, NS, SK])
        probs = sb("probs", [P, NP, SK])
        neg_max = sb("neg_max", [P, NCOL])
        sums = sb("sums", [P, NCOL])
        rsum = sb("rsum", [P, NCOL])
        probsT = sb("probsT", [P, 2, 4, NK, SQ])
        mixT = sb("mixT", [P, 2, TOK])
        wT = sb("wT", [P, 3, 4, P])
        val = sb("val", [P, 2, NC, P])

        w0 = sb("w0", [P, 4, 4, P])
        wo0 = sb("wo0", [P, P])
        bq0 = sb("bq0", [P, 4])
        bk0 = sb("bk0", [P, 4])
        bv0 = sb("bv0", [P, P])
        bo0 = sb("bo0", [P, P])
        m0_u8 = sb("m0_u8", [P, NQ, SK], U8)
        mask0 = sb("mask0", [P, NQ, SK], BF16)
        full0 = sb("full0", [P, SK])
        high0 = sb("high0", [P, SK], F32R)
        qst0 = sb("qst0", [P, TOK])
        k0 = sb("k0", [P, 2, B * SK], F32R)
        q0 = sb("q0", [P, 2, 4, TOK], F32R)
        w1 = sb("w1", [P, 8, 4, P])
        bq1 = sb("bq1", [P, 8])
        bk1 = sb("bk1", [P, 8])
        bv1 = sb("bv1", [P, 8 * P])
        bo1 = sb("bo1", [P, P])
        m1_u8 = sb("m1_u8", [P, B, NQ, SK], U8)
        mask1 = sb("mask1", [P, B, NQ, SK], BF16)
        k1 = sb("k1", [P, 2, B * SK])
        q1 = sb("q1", [P, 2, 2, TOK])
        fw = sb("fw", [P, P])
        fq = sb("fq", [P, P])
        fcol = sb("fcol", [P, 4])
        fwT = sb("fwT", [P, P])
        xh, xq = (masked[:, i, :].rearrange("p (t c) -> p t c", c=P) for i in range(2))
        xqT = masked[:, 2, :]
        qs = sb("qs", [P, 3, NT])
        wg = sb("wg", [P, EXPERTS])
        we1 = sb("we1", [P, PAIRS + 1, P])
        we3 = sb("we3", [P, PAIRS + 1, P])
        we2 = sb("we2", [P, PAIRS + 1, P])
        lg = sb("lg", [P, NT])
        ls = sb("ls", [P, NT])
        lr = sb("lr", [P, NT])
        ex = sb("ex", [P, NT, EXPERTS])
        sc = sb("sc", [P, NT, EXPERTS])
        top8 = sb("top8", [P, NT, 8])
        above = sb("above", [P, NT, EXPERTS])
        equal = sb("equal", [P, NT, EXPERTS])
        run = sb("run", [P, NT, EXPERTS])
        room = sb("room", [P, NT])
        sel = sb("sel", [P, NT, EXPERTS])
        sel_b = sb("sel_b", [P, NT, EXPERTS], BF16)
        kept = sb("kept", [P, NT, EXPERTS])
        wgt = sb("wgt", [P, NT, 2, EXPERTS])
        ones32 = sb("ones32", [P, EXPERTS])
        ones_b = sb("ones_b", [P, P], BF16)
        before_b = sb("before_b", [P, P], BF16)
        gate_hi, gate_full = high0[0:2 * EXPERTS, :], full0[0:2 * EXPERTS, :]
        gateT = q0[:, 0, 0, :]
        spread_f = w0[:, :, :, :].rearrange("p g a c -> p (g a c)").rearrange("p (e h) -> p e h", h=HID)
        spread = k0[:, :, :].rearrange("p a k -> p (a k)").rearrange("p (e h) -> p e h", h=HID)
        flat = probsT[:, :, :, :, :].rearrange("p a h k q -> p (a h k q)")
        silu, prod, hidT = (flat[:, 2 * TOK * i:2 * TOK * (i + 1)].rearrange("p (i t) -> p i t", i=2) for i in range(3))

        ld = {n: sem("ld_" + n) for n in (
            "x", "ctx", "g", "had", "w0", "wo0", "b0", "bv0", "m0", "w1", "b1", "bv1", "m1", "fw", "moe")}
        const_ready = sem("const_ready")
        pool_step = sem("pool_step")
        mask_ready = [sem("mask0_ready"), sem("mask1_ready")]
        tanh_ready = sem("tanh_ready")
        ctx_turned = sem("ctx_turned")
        ctxT_ready = sem("ctxT_ready")
        dve_step = sem("dve_step")
        var_ready = sem("var_ready")
        rstd_ready = sem("rstd_ready")
        xn_ready = sem("xn_ready")
        xn_turned = sem("xn_turned")
        xnT_ready = sem("xnT_ready")
        fw_ready = sem("fw_ready")
        fw_turned = sem("fw_turned")
        fwT_ready = sem("fwT_ready")
        rot_ready = sem("rot_ready")
        rot_copied = sem("rot_copied")
        xq_ready = sem("xq_ready")
        xq_turned = sem("xq_turned")
        xqT_ready = sem("xqT_ready")
        ffn_ready = sem("ffn_ready")
        y_used = sem("y_used")
        logit_ready = sem("logit_ready")
        lmax_ready = sem("lmax_ready")
        lexp_ready = sem("lexp_ready")
        sel_ready = sem("sel_ready")
        rank_ready = sem("rank_ready")
        wgt_ready = sem("wgt_ready")
        gate_turned = sem("gate_turned")
        gate_copied = sem("gate_copied")
        gateT_ready = sem("gateT_ready")
        u_ready = sem("u_ready")
        v_ready = sem("v_ready")
        g_ready = sem("g_ready")
        silu_ready = sem("silu_ready")
        prod_ready = sem("prod_ready")
        hid_ready = sem("hid_ready")
        down_done = sem("down_done")
        stored = sem("stored")

        class Attention:

            def __init__(self, n, groups, heads, width, depth, lead, offsets):
                self.n, self.groups, self.heads, self.width, self.lead = n, groups, heads, width, lead
                self.scale = float(depth) ** -0.5
                self.batch_units = heads * NQ
                self.units = B * self.batch_units
                self.total = groups * self.units
                self.offsets = dict(zip(JOBS, offsets))
                self.w = (w0, w1)[n]
                self.k, self.q = ((k0, q0), (k1, q1))[n]
                self.bq, self.bk, self.bv = ((bq0, bk0, bv0), (bq1, bk1, bv1))[n]
                self.scored = sem(f"a{n}_scored")
                self.maxed = sem(f"a{n}_maxed")
                self.exped = sem(f"a{n}_exped")
                self.recipped = sem(f"a{n}_recipped")
                self.normed = sem(f"a{n}_normed")
                self.turned = sem(f"a{n}_turned")
                self.copied_act = sem(f"a{n}_copied_act")
                self.copied_dve = sem(f"a{n}_copied_dve")
                self.mixed = sem(f"a{n}_mixed")
                self.mix_copied = sem(f"a{n}_mix_copied")
                self.projected_out = sem(f"a{n}_projected_out")
                self.job_done = sem(f"a{n}_job_done")
                self.job_copied_act = sem(f"a{n}_job_copied_act")
                self.job_copied_dve = sem(f"a{n}_job_copied_dve")
                self.k_ready = sem(f"a{n}_k_ready")
                self.stack_ready = sem(f"a{n}_stack_ready")
                self.q_ready = sem(f"a{n}_q_ready")

        def unit(L, u):
            g, r = divmod(u, L.units)
            b, r = divmod(r, L.batch_units)
            h, qt = divmod(r, NQ)
            return g, b, h, qt

        A = [Attention(0, 4, 4, 32, 8, 4, (0, 2, 4, 6, 8, 9)),
             Attention(1, 8, 2, 64, 64, 3, (0, 1, 2, 3, 4, 5))]

        block = ctx.enter_context(nc.Block())

        @block.sync
        def _(sp):
            sp.dma_start(ctx_sb[:, :, :], a["ctx_1024"].rearrange("b (t p) d -> p (b t) d", p=P)).then_inc(ld["ctx"], 16)
            sp.dma_start(x_sb[:, :, :], a["x"].rearrange("b (t p) d -> p (b t) d", p=P)).then_inc(ld["x"], 16)
            wo = a["L0_xattn_Wo"]
            sp.dma_start(wo0[:, :], wo).then_inc(ld["wo0"], 16)
            for rep in range(4):
                r = slice(32 * rep, 32 * rep + 32)
                sp.dma_start(w0[r, :, 0, :], a["L0_xattn_Wq"].rearrange("(g p) d -> p g d", p=32)).then_inc(ld["w0"], 16)
                sp.dma_start(w0[r, :, 1, :], a["L0_xattn_Wk"].rearrange("(g p) d -> p g d", p=32)).then_inc(ld["w0"], 16)
            sp.wait_ge(const_ready, 1)
            for j in range(4):
                sp.dma_start(w0[32 * j:32 * j + 8, :, 2, :],
                             a["L0_xattn_Wv"].rearrange("(g j p) d -> j p g d", j=4, p=8)[j]).then_inc(ld["w0"], 16)
            sp.dma_start(m0_u8[:, :, :], a["mask_1x1xSxS2_bk0"].rearrange("a c (t p) k -> p (a c t) k", p=P)).then_inc(ld["m0"], 16)
            sp.dma_start(fw[:, :], a["L0_ffn_weight"]).then_inc(ld["fw"], 16)
            sp.dma_start(had[:, :], a["hadamard"]).then_inc(ld["had"], 16)
            for i, name in enumerate(("L1_xattn_W_Q", "L1_xattn_W_K", "L1_xattn_W_V")):
                sp.dma_start(w1[:, :, i, :], a[name].rearrange("(g p) d -> p g d", p=P)).then_inc(ld["w1"], 16)
            sp.dma_start(w1[:, :, 3, :], a["L1_xattn_W_out"].rearrange("o (g c) -> o g c", c=P)).then_inc(ld["w1"], 16)
            sp.dma_start(m1_u8[:, :, :, :].rearrange("p b t k -> p (b t) k"),
                         a["mask_BxSxS2_bk1"].rearrange("b (t p) k -> p (b t) k", p=P)).then_inc(ld["m1"], 16)
            sp.dma_start(wg[:, :], a["L1_ffn_Wg"]).then_inc(ld["moe"], 16)
            for s, w, shared in ((we1, "L1_ffn_W1", "L1_ffn_Ws1"), (we3, "L1_ffn_W3", "L1_ffn_Ws3")):
                sp.dma_start(s[:, 0:PAIRS, :].rearrange("p q (e h) -> p (q e) h", h=HID),
                             a[w].rearrange("e d h -> d e h")).then_inc(ld["moe"], 16)
                sp.dma_start(s[:, PAIRS, :], a[shared]).then_inc(ld["moe"], 16)
            sp.dma_start(we2[:, 0:PAIRS, :], a["L1_ffn_W2"].rearrange("(q e) h d -> (e h) q d", e=2)).then_inc(ld["moe"], 16)
            sp.dma_start(we2[:, PAIRS, :], a["L1_ffn_Ws2"]).then_inc(ld["moe"], 16)
            sp.wait_ge(y_used, 4)
            sp.dma_start(out.rearrange("b (t p) d -> p (b t) d", p=P), x_sb[:, :, :]).then_inc(stored, 16)
            sp.wait_ge(stored, 16)

        @block.gpsimd
        def _(pool):
            done = [0]

            def step(ins):
                done[0] += 1
                ins.then_inc(pool_step, 1)
                pool.wait_ge(pool_step, done[0])

            told = [0]

            def publish(ins):
                told[0] += 1
                ins.then_inc(const_ready, 1)
                pool.wait_ge(const_ready, told[0])

            publish(pool.memset(w0[:, :, 2:4, :], 0.0))
            step(pool.memset(ident[:, :], 0.0))
            publish(pool.affine_select(out=ident[:, :], in_=ident[:, :], compare_op=ALU.not_equal, fill=1.0, base=0,
                               pattern=[[-1, P]], channel_multiplier=1))
            for r, signs in ((32, (0.0, 0.0)), (64, (-1.0, 0.0)), (96, (0.0, -1.0)), (128, (-1.0, -1.0))):
                rows = slice(r - 32, r)
                publish(pool.memset(lo_k[rows, :], signs[0]))
                publish(pool.memset(lo_q[rows, :], signs[1]))
            step(pool.memset(head_row[:, :], 1.0))
            for r in range(4):
                rows = head_row[32 * r:32 * r + 32, :]
                step(pool.affine_select(out=rows, in_=rows, compare_op=ALU.is_ge, fill=0.0, base=0,
                                        pattern=[[-8, 4]], channel_multiplier=1))
                publish(pool.affine_select(out=rows, in_=rows, compare_op=ALU.is_ge, fill=0.0, base=7,
                                           pattern=[[8, 4]], channel_multiplier=-1))
            publish(pool.memset(q1[64:P, :, 0, :], 0.0))
            publish(pool.memset(q1[0:64, :, 1, :], 0.0))
            publish(pool.memset(val[:, :, :, :], 0.0))
            publish(pool.memset(neg_half[:, :], -0.5))
            pool.wait_ge(ld["wo0"], 16)
            step(pool.tensor_copy(w0[:, :, 3, :].rearrange("p g (j c) -> p g j c", c=32)[:, :, :, 0:8],
                                  wo0[:, :].rearrange("p (g j c) -> p g j c", j=4, c=8)))
            pool.wait_ge(ld["m0"], 16)
            pool.tensor_scalar(mask0[:, :, :], m0_u8[:, :, :], FAR, -FAR, ALU.mult, ALU.add).then_inc(mask_ready[0], 1)

            def ln_rstd(n):
                pool.wait_ge(var_ready, n + 1)
                pool.tensor_tensor(rstd[:, :], veps[:, :], neg_half[:, :], ALU.pow).then_inc(rstd_ready, 1)

            def norm(L, u):
                pool.wait_ge(L.recipped, u + 1)
                p = probs[:, u % NP, :]
                pool.tensor_scalar(p, p, rsum[:, u % NCOL:u % NCOL + 1], 1.0, ALU.mult, ALU.mult).then_inc(L.normed, 1)

            def q_stack(g):
                L = A[0]
                pool.wait_ge(L.stack_ready, g + 1)
                if g >= 2:
                    pool.wait_ge(L.scored, L.units * (g - 1))
                for j in range(4):
                    pool.tensor_scalar(q0[:, g % 2, j, :], qst0[:, :], head_row[:, j:j + 1], 1.0,
                                       ALU.mult, ALU.mult).then_inc(L.q_ready, 1)

            ln_rstd(0)
            q_stack(0)
            L = A[0]
            for t in range(-L.lead, L.total):
                if 0 <= t + 2 < L.total:
                    norm(L, t + 2)
                if t >= 0 and t % L.units == L.offsets["q"] and t // L.units + 1 < L.groups:
                    q_stack(t // L.units + 1)
            pool.wait_ge(ld["m1"], 16)
            pool.tensor_scalar(mask1[:, :, :, :], m1_u8[:, :, :, :], -FAR, 0.0, ALU.mult, ALU.add).then_inc(mask_ready[1], 1)
            ln_rstd(1)
            ln_rstd(2)
            L = A[1]
            for u in range(L.total):
                norm(L, u)
            step(pool.memset(spread_f[:, :, :], 0.0))
            for half in range(2):
                rows = spread_f[32 * half:32 * half + 32, :, :]
                step(pool.affine_select(out=rows, in_=rows, compare_op=ALU.not_equal, fill=1.0, base=0,
                                        pattern=[[-1, EXPERTS], [0, HID]], channel_multiplier=1))
            step(pool.memset(ones32[:, :], 1.0))
            step(pool.memset(gateT[64:P, :].bitcast(F32), 0.0))
            step(pool.memset(before_b[:, :], 0.0))
            step(pool.memset(ones_b[:, :], 1.0))
            pool.affine_select(out=before_b[:, :], in_=ones_b[:, :], compare_op=ALU.is_gt, fill=0.0, base=0,
                               pattern=[[1, P]], channel_multiplier=-1).then_inc(const_ready, 1)
            ln_rstd(3)

        @block.scalar
        def _(act):
            act.dma_start(bv0[:, :], a["L0_xattn_bv"].partition_broadcast(P)).then_inc(ld["bv0"], 16)
            for r in range(4):
                rows = slice(32 * r, 32 * r + 32)
                act.dma_start(bq0[rows, :], a["L0_xattn_bq"].rearrange("(g p) -> p g", p=32), allow_slow_non_contiguous=True).then_inc(ld["b0"], 16)
                act.dma_start(bk0[rows, :], a["L0_xattn_bk"].rearrange("(g p) -> p g", p=32), allow_slow_non_contiguous=True).then_inc(ld["b0"], 16)
            act.dma_start(bo0[:, :], a["L0_xattn_bo"].partition_broadcast(P)).then_inc(ld["bv0"], 16)
            act.dma_start(gates[:, 0:2], a["g_xattn"].partition_broadcast(P)).then_inc(ld["g"], 16)
            act.dma_start(gates[:, 2:4], a["g_ffn"].partition_broadcast(P)).then_inc(ld["g"], 16)
            act.dma_start(bq1[:, :], a["L1_xattn_b_Q"].rearrange("(g p) -> p g", p=P), allow_slow_non_contiguous=True).then_inc(ld["b1"], 16)
            act.dma_start(bk1[:, :], a["L1_xattn_b_K"].rearrange("(g p) -> p g", p=P), allow_slow_non_contiguous=True).then_inc(ld["b1"], 16)
            act.dma_start(bv1[:, :], a["L1_xattn_b_V"].partition_broadcast(P)).then_inc(ld["bv1"], 16)
            act.dma_start(bo1[:, :], a["L1_xattn_b_out"].partition_broadcast(P)).then_inc(ld["bv1"], 16)
            for i in range(2):
                act.wait_ge(ctx_turned, i + 1)
                act.activation(ctxT[:, 512 * i:512 * i + 512], turn_bank[i][:, :], ACT.Copy).then_inc(ctxT_ready, 1)
            act.wait_ge(ld["g"], 32)
            act.activation(tanh_g[:, :], gates[:, :], ACT.Tanh).then_inc(tanh_ready, 1)

            def ln_copy(n):
                act.wait_ge(xn_turned, n + 1)
                act.activation(xnT[:, :], job_bank[:, :], ACT.Copy).then_inc(xnT_ready, 1)

            def exp(L, u):
                act.wait_ge(L.maxed, u + 1)
                if u >= NP:
                    act.wait_ge(L.turned, u - NP + 1)
                if u >= NCOL:
                    act.wait_ge(L.recipped, u - NCOL + 1)
                c = u % NCOL
                act.activation(probs[:, u % NP, :], masked[:, u % NS, :], ACT.Exp, scale=-1.0,
                               bias=neg_max[:, c:c + 1], accum_out=sums[:, c:c + 1]).then_inc(L.exped, 1)

            def copy_turned(L, u):
                g, b, h, qt = unit(L, u)
                m = B * g + b
                act.wait_ge(L.turned, u + 1)
                if m >= 2:
                    act.wait_ge(L.mixed, m - 1)
                act.activation(probsT[:, m % 2, h, :, qt * P:qt * P + P],
                               turn_bank[0][:, :].rearrange("p (k q) -> p k q", q=P), ACT.Copy).then_inc(L.copied_act, 1)

            def job_copy(L, job, g):
                i = JOBS.index(job)
                if i >= 4:
                    return
                act.wait_ge(L.job_done, 6 * g + i + 1)
                if job == "weights":
                    if g >= 3:
                        act.wait_ge(L.projected_out, g - 2)
                    act.activation(wT[:, g % 3, :, :].rearrange("p a c -> p (a c)"), job_bank[:, :],
                                   ACT.Copy).then_inc(L.job_copied_act, 1)
                    return
                if g >= 2:
                    act.wait_ge(L.scored, L.units * (g - 1))
                bias = (L.bq if job == "q" else L.bk)[:, g:g + 1]
                if L.n == 0:
                    if job == "k1":
                        act.wait_ge(L.stack_ready, g + 1)
                    elif job == "q":
                        act.wait_ge(L.k_ready, 2 * g + 1)
                    elif g >= 1:
                        act.wait_ge(L.k_ready, 2 * g)
                    act.activation(full0[:, :], job_bank[:, :], ACT.Identity, bias=bias).then_inc(L.job_copied_act, 1)
                    act.activation(high0[:, :], job_bank[:, :], ACT.Identity, bias=bias).then_inc(L.job_copied_act, 1)
                elif job == "q":
                    for h in range(2):
                        rows = slice(64 * h, 64 * h + 64)
                        act.activation(L.q[rows, g % 2, h, :], job_bank[rows, :], ACT.Identity,
                                       bias=L.bq[rows, g:g + 1]).then_inc(L.job_copied_act, 1)
                else:
                    b = int(job[1])
                    act.activation(L.k[:, g % 2, b * SK:b * SK + SK], job_bank[:, :], ACT.Identity,
                                   bias=bias).then_inc(L.job_copied_act, 1)

            def mix_copy(L, g):
                act.wait_ge(L.mixed, B * g + B)
                if g >= 2:
                    act.wait_ge(L.projected_out, g - 1)
                act.activation(mixT[:, g % 2, :], mix_bank[:, :], ACT.Copy).then_inc(L.mix_copied, 1)

            def attention_part(L):
                for t in range(-L.lead, L.total + 3):
                    if 0 <= t + L.lead - 1 < L.total:
                        exp(L, t + L.lead - 1)
                    if 0 <= t < L.total and t % 2 == 0:
                        copy_turned(L, t)
                    g, o = divmod(t, L.units)
                    if t >= L.units and o == 2:
                        mix_copy(L, g - 1)
                    if t >= 0 and g + 1 < L.groups:
                        for job in JOBS:
                            if L.offsets[job] == o:
                                job_copy(L, job, g + 1)

            act.wait_ge(ld["b0"], 16 * 8)
            for job in ("weights", "k0"):
                job_copy(A[0], job, 0)
            ln_copy(0)
            for job in ("q", "k1"):
                job_copy(A[0], job, 0)
            attention_part(A[0])
            act.wait_ge(fw_turned, 1)
            act.activation(fwT[:, :], turn_bank[0][:, 0:P], ACT.Copy).then_inc(fwT_ready, 1)
            ln_copy(1)
            act.wait_ge(rot_ready, 1)
            act.activation(masked[:, 0, :], job_bank[:, :], ACT.Copy).then_inc(rot_copied, 1)
            act.wait_ge(xq_turned, 1)
            act.activation(xqT, turn_bank[1][:, :], ACT.Copy).then_inc(xqT_ready, 1)
            act.wait_ge(ld["b1"], 32)
            act.wait_ge(const_ready, 18)
            for job in ("weights", "k0"):
                job_copy(A[1], job, 0)
            ln_copy(2)
            for job in ("q", "k1"):
                job_copy(A[1], job, 0)
            attention_part(A[1])
            ln_copy(3)
            act.wait_ge(lmax_ready, 1)
            act.wait_ge(logit_ready, 1)
            for t in range(NT):
                act.activation(ex[:, t, :], y_bank[:, t * EXPERTS:(t + 1) * EXPERTS], ACT.Exp, bias=lg[:, t:t + 1],
                               accum_out=ls[:, t:t + 1]).then_inc(lexp_ready, 1)
            act.wait_ge(gate_turned, 1)
            act.activation(gate_full, turn_bank[0][0:2 * EXPERTS, :], ACT.Copy).then_inc(gate_copied, 1)
            act.activation(gate_hi, turn_bank[0][0:2 * EXPERTS, :], ACT.Copy).then_inc(gate_copied, 1)
            for p in range(PAIRS + 1):
                act.wait_ge(u_ready, p + 1)
                if p >= 2:
                    act.wait_ge(prod_ready, p - 1)
                act.activation(silu[:, p % 2, :], bank[p % 2][:, :], ACT.Silu).then_inc(silu_ready, 1)

        @block.vector
        def _(dve):
            done = [0]

            def step(ins):
                done[0] += 1
                ins.then_inc(dve_step, 1)
                dve.wait_ge(dve_step, done[0])

            def layer_norm(n):
                for t in range(NT):
                    step(dve.bn_stats(stats[:, t, :], x_sb[:, t, :]))
                for t in range(NT):
                    step(dve.bn_aggr(mv[:, t, :], stats[:, t, :]))
                dve.tensor_scalar(veps[:, :], mv[:, :, 1], LN_EPS, None, ALU.add).then_inc(var_ready, 1)
                dve.wait_ge(rstd_ready, n + 1)
                if n >= 1:
                    dve.wait_ge(xn_turned, n)
                for t in range(NT):
                    dve.tensor_scalar(xn[:, t, :], x_sb[:, t, :], mv[:, t, 0:1], rstd[:, t:t + 1],
                                      ALU.subtract, ALU.mult).then_inc(xn_ready, 1)

            def add_y(n, bias):
                gate = tanh_g[:, (0, 2, 1, 3)[n]:(0, 2, 1, 3)[n] + 1]
                y = y_bank[:, :].rearrange("p (t c) -> p t c", c=P)
                if bias is not None:
                    b = bias[:, :].unsqueeze(1).to_broadcast([P, NT, P])
                    step(dve.tensor_tensor(tmp[:, :, :], y, b, ALU.add))
                    y = tmp[:, :, :]
                ins = dve.scalar_tensor_tensor(out=x_sb[:, :, :], in0=y, scalar=gate, in1=x_sb[:, :, :],
                                               op0=ALU.mult, op1=ALU.add)
                done[0] += 1
                ins.then_inc(y_used, 1)
                dve.wait_ge(y_used, n + 1)
                done[0] -= 1

            def mask_max(L, u):
                g, b, h, qt = unit(L, u)
                dve.wait_ge(L.scored, u + 1)
                if u >= NS:
                    dve.wait_ge(L.exped, u - NS + 1)
                mask = mask0[:, qt, :] if L.n == 0 else mask1[:, b, qt, :]
                c = u % NCOL
                dve.tensor_tensor_reduce(out=masked[:, u % NS, :], in0=score_bank[u % 3][:, :], in1=mask,
                                         scale=-L.scale, scalar=3.0e38, op0=ALU.add, op1=ALU.min,
                                         accum_out=neg_max[:, c:c + 1]).then_inc(L.maxed, 1)

            def recip(L, u):
                c = u % NCOL
                dve.wait_ge(L.exped, u + 1)
                if u >= NCOL:
                    dve.wait_ge(L.normed, u - NCOL + 1)
                dve.reciprocal(rsum[:, c:c + 1], sums[:, c:c + 1]).then_inc(L.recipped, 1)

            def copy_turned(L, u):
                g, b, h, qt = unit(L, u)
                m = B * g + b
                dve.wait_ge(L.turned, u + 1)
                if m >= 2:
                    dve.wait_ge(L.mixed, m - 1)
                dve.tensor_copy(probsT[:, m % 2, h, :, qt * P:qt * P + P],
                                turn_bank[1][:, :].rearrange("p (k q) -> p k q", q=P)).then_inc(L.copied_dve, 1)

            def job_copy(L, job, g):
                i = JOBS.index(job)
                if i >= 4:
                    b = int(job[1])
                    dve.wait_ge(L.job_done, 6 * g + i + 1)
                    if g >= 2:
                        dve.wait_ge(L.mixed, B * (g - 1))
                    if L.n == 0:
                        dst = val[:, g % 2, NK * b:NK * b + NK, :].rearrange("p k (j c) -> p k j c", c=32)[:, :, :, 0:8]
                        src = job_bank[:, :].rearrange("p (k j c) -> p k j c", j=4, c=32)[:, :, :, 0:8]
                        bias = bv0[:, 32 * g:32 * g + 32].rearrange("p (j c) -> p j c", c=8).unsqueeze(1)\
                            .to_broadcast([P, NK, 4, 8])
                    else:
                        dst = val[:, g % 2, NK * b:NK * b + NK, :]
                        src = job_bank[:, :].rearrange("p (k c) -> p k c", c=P)
                        bias = bv1[:, P * g:P * g + P].unsqueeze(1).to_broadcast([P, NK, P])
                    dve.tensor_tensor(dst, src, bias, ALU.add).then_inc(L.job_copied_dve, 1)
                elif L.n == 0 and i >= 1:
                    dve.wait_ge(L.job_copied_act, 7 * g + 1 + 2 * i)
                    if job == "q":
                        if g >= 1:
                            dve.wait_ge(L.q_ready, 4 * g)
                        dst, sign = qst0[:, :], lo_q
                    else:
                        b = int(job[1])
                        dst, sign = L.k[:, g % 2, b * SK:b * SK + SK], lo_k
                    dve.scalar_tensor_tensor(out=dst, in0=high0[:, :].bitcast(F32), scalar=sign[:, 0:1], in1=full0[:, :],
                                             op0=ALU.mult, op1=ALU.add)\
                       .then_inc(L.stack_ready if job == "q" else L.k_ready, 1)

            def attention_part(L):
                for t in range(-L.lead, L.total + 3):
                    if 0 <= t + L.lead - 1 < L.total:
                        mask_max(L, t + L.lead - 1)
                    if 0 <= t + L.lead - 2 < L.total:
                        recip(L, t + L.lead - 2)
                    if 0 <= t < L.total and t % 2 == 1:
                        copy_turned(L, t)
                    g, o = divmod(t, L.units)
                    if t >= 0 and g + 1 < L.groups:
                        for job in JOBS:
                            if L.offsets[job] == o:
                                job_copy(L, job, g + 1)

            dve.wait_ge(ld["x"], 16)
            dve.wait_ge(const_ready, 18)
            dve.wait_ge(ld["bv0"], 32)
            job_copy(A[0], "k0", 0)
            layer_norm(0)
            for job in ("q", "k1", "v0", "v1"):
                job_copy(A[0], job, 0)
            dve.wait_ge(mask_ready[0], 1)
            attention_part(A[0])
            dve.wait_ge(A[0].projected_out, A[0].groups)
            dve.wait_ge(tanh_ready, 1)
            add_y(0, bo0)
            dve.wait_ge(ld["fw"], 16)
            step(dve.tensor_reduce(fcol[:, 0:1], fw[:, :], X, ALU.add, apply_absolute_value=True))
            step(dve.tensor_scalar(fcol[:, 1:2], fcol[:, 0:1], 1.0 / P, 1e-5, ALU.mult, ALU.max))
            step(dve.reciprocal(fcol[:, 2:3], fcol[:, 1:2]))
            step(dve.tensor_scalar(fq[:, :], fw[:, :], fcol[:, 2:3], None, ALU.mult))
            step(dve.tensor_scalar(tmp[:, 0, :], fq[:, :], 0.5, None, ALU.is_gt))
            step(dve.tensor_scalar(tmp[:, 1, :], fq[:, :], -0.5, None, ALU.is_lt))
            step(dve.tensor_tensor(tmp[:, 0, :], tmp[:, 0, :], tmp[:, 1, :], ALU.subtract))
            step(dve.scalar_tensor_tensor(out=tmp[:, 1, :], in0=tmp[:, 0, :], scalar=fcol[:, 1:2], in1=fw[:, :],
                                          op0=ALU.mult, op1=ALU.subtract))
            dve.tensor_tensor(fq[:, :], fw[:, :], tmp[:, 1, :], ALU.add).then_inc(fw_ready, 1)
            layer_norm(1)
            dve.wait_ge(rot_copied, 1)
            step(dve.tensor_reduce(qs[:, 0, :], xh[:, :, :], X, ALU.max, apply_absolute_value=True))
            step(dve.tensor_scalar(qs[:, 1, :], qs[:, 0, :], 1e-5, 1.0 / 7.0, ALU.max, ALU.mult))
            step(dve.reciprocal(qs[:, 2, :], qs[:, 1, :]))
            inv = qs[:, 2, :].unsqueeze(2).to_broadcast([P, NT, P])
            scl = qs[:, 1, :].unsqueeze(2).to_broadcast([P, NT, P])
            ROUND = 1.5 * 2.0 ** 23
            step(dve.tensor_tensor(tmp[:, :, :], xh[:, :, :], inv, ALU.mult))
            step(dve.tensor_scalar(tmp[:, :, :], tmp[:, :, :], ROUND, -ROUND, ALU.add, ALU.add))
            step(dve.tensor_scalar(tmp[:, :, :], tmp[:, :, :], -8.0, 7.0, ALU.max, ALU.min))
            step(dve.tensor_tensor(tmp[:, :, :], tmp[:, :, :], scl, ALU.mult))
            step(dve.tensor_tensor(tmp[:, :, :], tmp[:, :, :], xh[:, :, :], ALU.subtract))
            dve.tensor_tensor(xq[:, :, :], xh[:, :, :], tmp[:, :, :], ALU.add).then_inc(xq_ready, 1)
            dve.wait_ge(ffn_ready, 1)
            dve.wait_ge(xq_ready, 1)
            add_y(1, None)
            layer_norm(2)
            dve.wait_ge(ld["bv1"], 32)
            for job in ("v0", "v1"):
                job_copy(A[1], job, 0)
            dve.wait_ge(mask_ready[1], 1)
            attention_part(A[1])
            dve.wait_ge(A[1].projected_out, A[1].groups)
            add_y(2, bo1)
            layer_norm(3)
            dve.wait_ge(const_ready, 19)
            dve.wait_ge(logit_ready, 1)
            logits = y_bank[:, 0:NT * EXPERTS].rearrange("p (t e) -> p t e", e=EXPERTS)
            dve.tensor_reduce(lg[:, :], logits, X, ALU.max, negate=True).then_inc(lmax_ready, 1)
            step(dve.tensor_copy(spread[:, :, :], spread_f[:, :, :]))
            dve.wait_ge(lexp_ready, NT)
            step(dve.reciprocal(lr[:, :], ls[:, :]))
            step(dve.tensor_tensor(sc[:, :, :], ex[:, :, :], lr[:, :].unsqueeze(2).to_broadcast([P, NT, EXPERTS]), ALU.mult))
            for t in range(NT):
                step(dve.max(top8[:, t, :], sc[:, t, :]))
            fourth = top8[:, :, TOP - 1:TOP].to_broadcast([P, NT, EXPERTS])
            step(dve.tensor_tensor(above[:, :, :], sc[:, :, :], fourth, ALU.is_gt))
            step(dve.tensor_tensor(equal[:, :, :], sc[:, :, :], fourth, ALU.is_equal))
            step(dve.tensor_reduce(lg[:, :], above[:, :, :], X, ALU.add))
            step(dve.tensor_scalar(room[:, :], lg[:, :], -1.0, float(TOP), ALU.mult, ALU.add))
            for t in range(NT):
                step(dve.tensor_tensor_scan(run[:, t, :], ones32[:, :], equal[:, t, :], 0.0, ALU.mult, ALU.add))
            step(dve.tensor_tensor(run[:, :, :], run[:, :, :], room[:, :].unsqueeze(2).to_broadcast([P, NT, EXPERTS]), ALU.is_le))
            step(dve.tensor_tensor(run[:, :, :], run[:, :, :], equal[:, :, :], ALU.mult))
            step(dve.tensor_tensor(sel[:, :, :], run[:, :, :], above[:, :, :], ALU.add))
            dve.tensor_copy(sel_b[:, :, :], sel[:, :, :]).then_inc(sel_ready, 1)
            dve.wait_ge(rank_ready, 1)
            rank = turn_bank[1][:, 0:NT * EXPERTS].rearrange("p (t e) -> p t e", e=EXPERTS)
            step(dve.scalar_tensor_tensor(out=kept[:, :, :], in0=rank, scalar=float(CAP), in1=sel[:, :, :],
                                          op0=ALU.is_lt, op1=ALU.mult))
            for i in range(2):
                dve.tensor_tensor(wgt[:, :, i, :], kept[:, :, :], sc[:, :, :], ALU.mult).then_inc(wgt_ready, 1)
            dve.wait_ge(gate_copied, 2)
            dve.scalar_tensor_tensor(out=gateT[0:2 * EXPERTS, :], in0=gate_hi.bitcast(F32),
                                     scalar=lo_k[0:2 * EXPERTS, 0:1], in1=gate_full,
                                     op0=ALU.mult, op1=ALU.add).then_inc(gateT_ready, 1)
            for p in range(PAIRS + 1):
                i = p % 2
                dve.wait_ge(silu_ready, p + 1)
                dve.wait_ge(v_ready, p + 1)
                if p >= 2:
                    dve.wait_ge(down_done, p - 1)
                if p < PAIRS:
                    dve.tensor_tensor(prod[:, i, :], bank[2 + i][:, :], silu[:, i, :], ALU.mult).then_inc(prod_ready, 1)
                    dve.wait_ge(g_ready, p + 1)
                    dve.wait_ge(prod_ready, p + 1)
                    dve.tensor_tensor(hidT[:, i, :], bank[4 + i][:, :], prod[:, i, :], ALU.mult).then_inc(hid_ready, 1)
                else:
                    dve.tensor_tensor(hidT[:, i, :], bank[2 + i][:, :], silu[:, i, :], ALU.mult).then_inc(hid_ready, 1)
            dve.wait_ge(down_done, PAIRS + 1)
            add_y(3, None)

        @block.tensor
        def _(pe):
            def transpose4(dst, src, n=4, rows=P):
                for t in range(n):
                    ins = pe.transpose(dst[0:rows, t * P:t * P + P], src(t), ident[:, :])
                return ins

            def ln_turn(n):
                pe.wait_ge(xn_ready, NT * (n + 1))
                transpose4(job_bank, lambda t: xn[:, t, :]).then_inc(xn_turned, 1)

            def job(L, name, g):
                i = JOBS.index(name)
                per = 7 if L.n == 0 else 5
                if i == 0:
                    if g >= 1:
                        pe.wait_ge(L.job_copied_dve, 2 * g)
                elif i <= 4:
                    copies = (0, 1, 3, 5, 7) if L.n == 0 else (0, 1, 2, 4, 5)
                    pe.wait_ge(L.job_copied_act, per * g + copies[i])
                else:
                    pe.wait_ge(L.job_copied_dve, 2 * g + 1)
                if name == "weights":
                    ins = transpose4(job_bank, lambda t: L.w[:, g, t, :])
                elif name == "q":
                    ins = pe.matmul(job_bank[:, :], wT[:, g % 3, 0, :], xnT[:, :], start=True, stop=True)
                elif name[0] == "k":
                    b = int(name[1])
                    ins = pe.matmul(job_bank[:, :], wT[:, g % 3, 1, :], ctxT[:, b * SK:b * SK + SK], start=True, stop=True)
                else:
                    b = int(name[1])
                    for k in range(NK):
                        ins = pe.matmul(job_bank[:, k * P:k * P + P], ctxT[:, (b * NK + k) * P:(b * NK + k + 1) * P],
                                        wT[:, g % 3, 2, :], start=True, stop=True)
                ins.then_inc(L.job_done, 1)

            def scores(L, u):
                g, b, h, qt = unit(L, u)
                if L.n == 0:
                    pe.wait_ge(L.k_ready, 2 * g + b + 1)
                    pe.wait_ge(L.q_ready, 4 * g + h + 1)
                else:
                    pe.wait_ge(L.job_copied_act, 5 * g + (4 if b == 0 else 5))
                if u >= 3:
                    pe.wait_ge(L.maxed, u - 2)
                col = b * SQ + qt * P
                pe.matmul(score_bank[u % 3][:, :], L.q[:, g % 2, h, col:col + P], L.k[:, g % 2, b * SK:b * SK + SK],
                          start=True, stop=True).then_inc(L.scored, 1)

            def turn(L, u):
                pe.wait_ge(L.normed, u + 1)
                if u >= 2:
                    pe.wait_ge(L.copied_dve if u % 2 else L.copied_act, u // 2)
                transpose4(turn_bank[u % 2], lambda t: probs[:, u % NP, t * P:t * P + P]).then_inc(L.turned, 1)

            def mix(L, m):
                g, b = divmod(m, B)
                pe.wait_ge(L.copied_act, (m + 1) * L.batch_units // 2)
                pe.wait_ge(L.copied_dve, (m + 1) * L.batch_units // 2)
                pe.wait_ge(L.job_copied_dve, m + 1)
                if b == 0 and g >= 1:
                    pe.wait_ge(L.mix_copied, g)
                w = L.width
                for k in range(NK):
                    for h in range(L.heads):
                        ins = pe.matmul(mix_bank[w * h:w * h + w, b * SQ:b * SQ + SQ],
                                        val[:, g % 2, b * NK + k, w * h:w * h + w],
                                        probsT[:, m % 2, h, k, :], start=(k == 0), stop=(k == NK - 1))
                ins.then_inc(L.mixed, 1)

            def project_out(L, g):
                pe.wait_ge(L.mix_copied, g + 1)
                for t in range(NT):
                    ins = pe.matmul(y_bank[:, t * P:t * P + P], mixT[:, g % 2, t * P:t * P + P], wT[:, g % 3, 3, :],
                                    start=(g == 0 and t == 0), stop=(g == L.groups - 1), skip_group_check=True)
                ins.then_inc(L.projected_out, 1)

            def attention_part(L):
                for t in range(-L.lead, L.total + 4):
                    if 0 <= t + L.lead < L.total:
                        scores(L, t + L.lead)
                    if 0 <= t < L.total:
                        turn(L, t)
                    m, o = divmod(t - 1, L.batch_units)
                    if t > 0 and o == 0 and m >= 1:
                        mix(L, m - 1)
                    g, o = divmod(t, L.units)
                    if g >= 1 and o == 3:
                        project_out(L, g - 1)
                    if t >= 0 and g + 1 < L.groups:
                        for name in JOBS:
                            if L.offsets[name] == o:
                                job(L, name, g + 1)

            pe.wait_ge(const_ready, 18)
            pe.wait_ge(pool_step, 7)
            pe.wait_ge(ld["w0"], 16 * 12)
            job(A[0], "weights", 0)
            pe.wait_ge(ld["ctx"], 16)
            for i in range(2):
                transpose4(turn_bank[i], lambda t: ctx_sb[:, 4 * i + t, :]).then_inc(ctx_turned, 1)
            pe.wait_ge(ctxT_ready, 2)
            job(A[0], "k0", 0)
            pe.wait_ge(A[0].job_copied_act, 3)
            ln_turn(0)
            pe.wait_ge(xnT_ready, 1)
            for name in ("q", "k1", "v0", "v1"):
                job(A[0], name, 0)
            attention_part(A[0])
            pe.wait_ge(fw_ready, 1)
            pe.transpose(turn_bank[0][:, 0:P], fq[:, :], ident[:, :]).then_inc(fw_turned, 1)
            ln_turn(1)
            pe.wait_ge(ld["had"], 16)
            pe.wait_ge(xnT_ready, 2)
            for t in range(NT):
                ins = pe.matmul(job_bank[:, t * P:t * P + P], xnT[:, t * P:t * P + P], had[:, :], start=True, stop=True)
            ins.then_inc(rot_ready, 1)
            pe.wait_ge(xq_ready, 1)
            transpose4(turn_bank[1], lambda t: xq[:, t, :]).then_inc(xq_turned, 1)
            pe.wait_ge(fwT_ready, 1)
            pe.wait_ge(xqT_ready, 1)
            pe.wait_ge(y_used, 1)
            for t in range(NT):
                ins = pe.matmul(y_bank[:, t * P:t * P + P], xqT[:, t * P:t * P + P], fwT[:, :], start=True, stop=True)
            ins.then_inc(ffn_ready, 1)
            pe.wait_ge(ld["w1"], 64)
            job(A[1], "weights", 0)
            job(A[1], "k0", 0)
            pe.wait_ge(A[1].job_copied_act, 2)
            ln_turn(2)
            pe.wait_ge(xnT_ready, 3)
            for name in ("q", "k1", "v0", "v1"):
                job(A[1], name, 0)
            pe.wait_ge(y_used, 2)
            attention_part(A[1])
            ln_turn(3)
            pe.wait_ge(ld["moe"], 16 * 7)
            pe.wait_ge(xnT_ready, 4)
            pe.wait_ge(y_used, 3)
            for t in range(NT):
                ins = pe.matmul(y_bank[:, t * EXPERTS:(t + 1) * EXPERTS], xnT[:, t * P:t * P + P], wg[:, :],
                                start=True, stop=True)
            ins.then_inc(logit_ready, 1)
            pe.wait_ge(sel_ready, 1)
            for t in range(NT):
                for s in range(t + 1):
                    ins = pe.matmul(turn_bank[1][:, t * EXPERTS:(t + 1) * EXPERTS],
                                    (before_b if s == t else ones_b)[:, :], sel_b[:, s, :],
                                    start=(s == 0), stop=(s == t))
            ins.then_inc(rank_ready, 1)
            pe.wait_ge(wgt_ready, 2)
            transpose4(turn_bank[0], lambda t: wgt[:, t, :, :].rearrange("p a e -> p (a e)"),
                       rows=2 * EXPERTS).then_inc(gate_turned, 1)
            pe.wait_ge(gateT_ready, 1)

            def down(p):
                pe.wait_ge(hid_ready, p + 1)
                for t in range(NT):
                    ins = pe.matmul(y_bank[:, t * P:t * P + P], hidT[:, p % 2, t * P:t * P + P], we2[:, p, :],
                                    start=(p == 0 and t == 0), stop=(p == PAIRS), skip_group_check=True)
                ins.then_inc(down_done, 1)

            for p in range(PAIRS + 1):
                i = p % 2
                if p >= 2:
                    pe.wait_ge(silu_ready, p - 1)
                pe.matmul(bank[i][:, :], we1[:, p, :], xnT[:, :], start=True, stop=True).then_inc(u_ready, 1)
                if p >= 2:
                    pe.wait_ge(hid_ready, p - 1)
                pe.matmul(bank[2 + i][:, :], we3[:, p, :], xnT[:, :], start=True, stop=True).then_inc(v_ready, 1)
                if p < PAIRS:
                    pe.matmul(bank[4 + i][:, :], spread[:, 2 * p:2 * p + 2, :].rearrange("p e h -> p (e h)"),
                              gateT, start=True, stop=True).then_inc(g_ready, 1)
                if p >= 1:
                    down(p - 1)
            down(PAIRS)


_INS = ["x", "ctx_1024", "mask_1x1xSxS2_bk0", "mask_BxSxS2_bk1", "g_xattn", "g_ffn", "L0_xattn_Wq", "L0_xattn_bq",
        "L0_xattn_Wk", "L0_xattn_bk", "L0_xattn_Wv", "L0_xattn_bv", "L0_xattn_Wo", "L0_xattn_bo", "L0_ffn_weight",
        "L1_xattn_W_Q", "L1_xattn_b_Q", "L1_xattn_W_K", "L1_xattn_b_K", "L1_xattn_W_V", "L1_xattn_b_V",
        "L1_xattn_W_out", "L1_xattn_b_out", "L1_ffn_Wg", "L1_ffn_W1", "L1_ffn_W2", "L1_ffn_W3", "L1_ffn_Ws1",
        "L1_ffn_Ws2", "L1_ffn_Ws3"]


def kernel(**inputs):
    import numpy as _np
    import concourse.bacc as _bacc
    from concourse import mybir as _mybir
    from concourse.bass_utils import run_bass_kernel_spmd as _run

    nc = _bacc.Bacc("TRN2", target_bir_lowering=False, num_devices=1)
    arrays, args = {}, {}

    def give(name, array):
        arrays[f"in_{name}"] = array
        args[name] = nc.dram_tensor(f"in_{name}", array.shape, _mybir.dt.from_np(array.dtype), kind="ExternalInput").ap()

    for name in _INS:
        give(name, _np.ascontiguousarray(inputs[name]))
    had = _np.array([[1.0]])
    while had.shape[0] < 128:
        had = _np.block([[had, had], [had, -had]])
    give("hadamard", (had / _np.sqrt(128)).astype(_np.float32))
    out = nc.dram_tensor("out_0", (2, 256, 128), _mybir.dt.float32, kind="ExternalOutput").ap()
    build(nc, args, out)
    r = _run(nc, [arrays], core_ids=[0])
    return r.results[0]["out_0"]
```

```python
import concourse.bass as bass
from concourse import mybir
from contextlib import ExitStack

F32 = mybir.dt.float32
F32R = mybir.dt.float32r
BF16 = mybir.dt.bfloat16
U8 = mybir.dt.uint8
ALU = mybir.AluOpType
ACT = mybir.ActivationFunctionType
X = mybir.AxisListType.X

P = 128
B, SQ, SK = 2, 256, 512
TOK = B * SQ
NT = TOK // P
NC = B * SK // P
NQ = SQ // P
NK = SK // P
LN_EPS = 1e-5
FAR = 1.7e38
EXPERTS, HID, TOP = 32, 64, 4
CAP = 4 * TOK * TOP // EXPERTS
PAIRS = EXPERTS // 2
HALVES = PAIRS + 1

LEAD = 5
NS, NP, NCOL = 3, 5, 8
NV = 3


class Block:

    def __init__(self, m, layer, b, g, first):
        self.m, self.layer, self.b, self.g, self.first = m, layer, b, g, first
        self.heads, self.width, self.depth = ((4, 32, 8), (2, 64, 64))[layer]
        self.groups = (4, 8)[layer]
        self.units = self.heads * NQ
        self.end = first + self.units


def make_blocks():
    blocks, first = [], 0
    for layer in range(2):
        for b in range(B):
            for g in range((4, 8)[layer]):
                blocks.append(Block(len(blocks), layer, b, g, first))
                first = blocks[-1].end
    return blocks


BLOCKS = make_blocks()
TOTAL = BLOCKS[-1].end
Y_DONE = {(k.layer, k.b): k.end + 4 for k in BLOCKS if k.g == k.groups - 1}


def make_plan():
    before = [("weights", 0), ("k", 0), ("ln", 0, 0), ("q", 0), ("v", 0)]
    plan = {}
    for k in BLOCKS[1:]:
        at = k.first - LEAD - 4
        for i, name in enumerate(("weights", "k", "q", "v")):
            if name != "weights" or k.b == 0:
                plan.setdefault(at + i, []).append((name, k.m))
    for b in range(B):
        s = Y_DONE[0, b]
        for o, job in ((3, ("ln", 1, b)), (5, ("rotate", b)), (9, ("turn_xq", b)), (11, ("ffn", b)),
                       (15, ("ln", 2, b))):
            plan.setdefault(s + o, []).append(job)
    route = ((3, "ln"), (5, "logits"), (9, "rank"), (11, "turn_gate"))
    for o, name in route:
        plan.setdefault(Y_DONE[1, 0] + o, []).append((name, 3, 0) if name == "ln" else (name, 0))
    after = {o: [(name, 3, 1) if name == "ln" else (name, 1)] for o, name in route}
    order = before + [j for t in sorted(plan) for j in plan[t]] + [j for o in sorted(after) for j in after[o]]
    number = {j: n for n, j in enumerate(order)}
    last = [j for o in after for j in after[o]]
    place, count = {}, [0, 0]
    for j in order:
        i = 1 if j in last else number[j] % 2
        place[j] = (i, count[i])
        count[i] += 1
    return before, plan, after, number, place


BEFORE, PLAN, AFTER, NUMBER, PLACE = make_plan()


def unit(u):
    k = [k for k in BLOCKS if k.first <= u < k.end][0]
    return (k, *divmod(u - k.first, NQ))


def build(nc, a, out):
    ctx = ExitStack()
    with ctx:
        def sb(name, shape, dt=F32):
            return ctx.enter_context(nc.sbuf_tensor(name, shape, dt))

        def sem(name):
            return ctx.enter_context(nc.semaphore(name))

        bank = [ctx.enter_context(nc.psum_tensor(f"bank{i}", [P, 512], F32)) for i in range(8)]
        score_bank = bank[0:2]
        turn_bank = bank[2:4]
        mix_bank, y_bank = bank[4], bank[7]
        job_banks = bank[5:7]

        ident = sb("ident", [P, P])
        had = sb("had", [P, P])
        lo_k = sb("lo_k", [P, 1])
        lo_q = sb("lo_q", [P, 1])
        head_row = sb("head_row", [P, 4])
        gates = sb("gates", [P, 4])
        tanh_g = sb("tanh_g", [P, 4])
        x_sb = sb("x_sb", [P, NT, P])
        ctx_sb = sb("ctx_sb", [P, NC, P])
        ctxT = sb("ctxT", [P, NC * P])

        xn = sb("xn", [P, NT, P])
        xnT = sb("xnT", [P, 3, TOK])
        stats = sb("stats", [P, NT, 6])
        mv = sb("mv", [P, NT, 2])
        veps = sb("veps", [P, NT])
        neg_half = sb("neg_half", [P, NT])
        rstd = sb("rstd", [P, NT])
        tmp = sb("tmp", [P, NQ, P])

        masked = sb("masked", [P, NS, SK])
        probs = sb("probs", [P, NP, SK])
        neg_max = sb("neg_max", [P, NCOL])
        sums = sb("sums", [P, NCOL])
        rsum = sb("rsum", [P, NCOL])
        probsT = sb("probsT", [P, 2, 4, NK, SQ])
        mixT = sb("mixT", [P, 2, SQ])
        val = sb("val", [P, NV, NK, P])
        full_k = sb("full_k", [P, SK])
        full_q = sb("full_q", [P, SQ])
        high_k = sb("high_k", [P, SK], F32R)
        high_q = sb("high_q", [P, SQ], F32R)
        stack_f = sb("stack_f", [P, SQ])

        w0 = sb("w0", [P, 4, 4, P])
        w0T = sb("w0T", [P, 4, 4, P])
        wo0 = sb("wo0", [P, P])
        bq0 = sb("bq0", [P, 4])
        bk0 = sb("bk0", [P, 4])
        bv0 = sb("bv0", [P, P])
        bo0 = sb("bo0", [P, P])
        m0_u8 = sb("m0_u8", [P, NQ, SK], U8)
        mask0 = sb("mask0", [P, NQ, SK], BF16)
        k0 = sb("k0", [P, 2, SK], F32R)
        q0 = sb("q0", [P, 2, 4, SQ], F32R)
        w1 = sb("w1", [P, 8, 4, P])
        w1T = sb("w1T", [P, 8, 4, P])
        bq1 = sb("bq1", [P, 8])
        bk1 = sb("bk1", [P, 8])
        bv1 = sb("bv1", [P, 8 * P])
        bo1 = sb("bo1", [P, P])
        m1_u8 = sb("m1_u8", [P, B, NQ, SK], U8)
        mask1 = sb("mask1", [P, B, NQ, SK], BF16)
        k1_high = sb("k1_high", [P, 2, 2, SK], F32R)
        k1_low = sb("k1_low", [P, 2, SK], F32R)
        q1_both = sb("q1_both", [P, 2, 2, SQ], F32R)
        q1_high = sb("q1_high", [P, 2, 2, SQ], F32R)
        fw = sb("fw", [P, P])
        fq = sb("fq", [P, P])
        fs = sb("fs", [P, 2, P])
        fcol = sb("fcol", [P, 4])
        fwT = sb("fwT", [P, P])
        xh = sb("xh", [P, NQ, P])
        xq = sb("xq", [P, NQ, P])
        xqT = sb("xqT", [P, SQ])
        qs = sb("qs", [P, 3, NQ])
        wg = sb("wg", [P, EXPERTS])
        we1 = sb("we1", [P, HALVES, P])
        we3 = sb("we3", [P, HALVES, P])
        lg = sb("lg", [P, NQ])
        ls = sb("ls", [P, NQ])
        lr = sb("lr", [P, NQ])
        ex = sb("ex", [P, NQ, EXPERTS])
        sc = sb("sc", [P, NQ, EXPERTS])
        top8 = sb("top8", [P, NQ, 8])
        above = sb("above", [P, NQ, EXPERTS])
        equal = sb("equal", [P, NQ, EXPERTS])
        run = sb("run", [P, NQ, EXPERTS])
        room = sb("room", [P, NQ])
        sel = sb("sel", [P, NQ, EXPERTS])
        sel_b = sb("sel_b", [P, NT, EXPERTS], BF16)
        kept = sb("kept", [P, NQ, EXPERTS])
        wgt = sb("wgt", [P, NQ, 2, EXPERTS])
        ones32 = sb("ones32", [P, EXPERTS])
        ones_b = sb("ones_b", [P, P], BF16)
        before_b = sb("before_b", [P, P], BF16)
        gate_hi = sb("gate_hi", [2 * EXPERTS, SQ], F32R)
        gate_full = sb("gate_full", [2 * EXPERTS, SQ])
        spread_f = w0[:, :, :, :].rearrange("p g a c -> p (g a c)").rearrange("p (e h) -> p e h", h=HID)
        spread = q0[:, :, :, :].rearrange("p i h t -> p (i h t)").rearrange("p (e h) -> p e h", h=HID)
        gateT = k0[:, 0, :]
        we2 = w1[:, :, :, :].rearrange("p g a c -> p (g a) c")[:, 0:HALVES, :]
        flat = probsT[:, :, :, :, :].rearrange("p a h k q -> p (a h k q)")
        silu, prod, hidT = (flat[:, 2 * SQ * i:2 * SQ * (i + 1)].rearrange("p (i t) -> p i t", i=2) for i in range(3))

        ld = {n: sem("ld_" + n) for n in (
            "x", "ctx0", "ctx1", "g", "had", "w0", "wo0", "b0", "bv0", "m0", "w1", "b1", "bv1", "m1", "fw", "moe")}
        zeros_ready = sem("zeros_ready")
        const_ready = sem("const_ready")
        pool_step = sem("pool_step")
        wo0_ready = sem("wo0_ready")
        late_ready = sem("late_ready")
        mask_ready = [sem("mask0_ready"), sem("mask1_ready")]
        tanh_ready = sem("tanh_ready")
        ctx_turned = sem("ctx_turned")
        ctxT_ready = sem("ctxT_ready")
        fw_ready = sem("fw_ready")
        fw_turned = sem("fw_turned")
        fwT_ready = sem("fwT_ready")
        dve_step = sem("dve_step")
        var_ready = sem("var_ready")
        rstd_ready = sem("rstd_ready")
        xn_ready = sem("xn_ready")
        scored = sem("scored")
        maxed = sem("maxed")
        exped = sem("exped")
        recipped = sem("recipped")
        normed = sem("normed")
        turned = sem("turned")
        copied_act = sem("copied_act")
        copied_dve = sem("copied_dve")
        mixed = sem("mixed")
        mix_copied = sem("mix_copied")
        projected_out = sem("projected_out")
        job_done = sem("job_done")
        job_free = [sem("job_free0"), sem("job_free1")]
        full_ready = sem("full_ready")
        half_done = sem("half_done")
        half_dve = sem("half_dve")
        k_ready = sem("k_ready")
        stack_ready = sem("stack_ready")
        q0_ready = sem("q0_ready")
        q1_ready = sem("q1_ready")
        y_used = sem("y_used")
        xq_ready = sem("xq_ready")
        lmax_ready = sem("lmax_ready")
        lexp_ready = sem("lexp_ready")
        sel_ready = sem("sel_ready")
        spread_ready = sem("spread_ready")
        wgt_ready = sem("wgt_ready")
        gate_copied = sem("gate_copied")
        gateT_ready = sem("gateT_ready")
        u_ready = sem("u_ready")
        v_ready = sem("v_ready")
        g_ready = sem("g_ready")
        silu_ready = sem("silu_ready")
        prod_ready = sem("prod_ready")
        hid_ready = sem("hid_ready")
        down_done = sem("down_done")
        stored = sem("stored")

        LN = {(0, 0): 0, (1, 0): 1, (2, 0): 2, (1, 1): 3, (2, 1): 4, (3, 0): 5, (3, 1): 6}

        def ln_tiles(n, b):
            return range(NT) if n == 0 else range(NQ * b, NQ * b + NQ)

        def xn_count(n, b):
            return NT + NQ * LN[n, b]

        def freed(job):
            return job_free[PLACE[job][0]], PLACE[job][1] + 1

        block = ctx.enter_context(nc.Block())

        @block.sync
        def _(sp):
            ctx_t = a["ctx_1024"].rearrange("b (t p) d -> p (b t) d", p=P)
            for r in range(4):
                sp.dma_start(w0[32 * r:32 * r + 32, :, 1, :],
                             a["L0_xattn_Wk"].rearrange("(g p) d -> p g d", p=32)).then_inc(ld["w0"], 16)
            sp.dma_start(ctx_sb[:, 0:4, :], ctx_t[:, 0:4, :]).then_inc(ld["ctx0"], 16)
            sp.dma_start(x_sb[:, :, :], a["x"].rearrange("b (t p) d -> p (b t) d", p=P)).then_inc(ld["x"], 16)
            sp.dma_start(ctx_sb[:, 4:8, :], ctx_t[:, 4:8, :]).then_inc(ld["ctx1"], 16)
            sp.dma_start(m0_u8[:, :, :], a["mask_1x1xSxS2_bk0"].rearrange("a c (t p) k -> p (a c t) k", p=P)).then_inc(ld["m0"], 16)
            sp.dma_start(fw[:, :], a["L0_ffn_weight"]).then_inc(ld["fw"], 16)
            sp.dma_start(had[:, :], a["hadamard"]).then_inc(ld["had"], 16)
            for i, name in enumerate(("L1_xattn_W_Q", "L1_xattn_W_K", "L1_xattn_W_V")):
                sp.dma_start(w1[:, :, i, :], a[name].rearrange("(g p) d -> p g d", p=P)).then_inc(ld["w1"], 16)
            sp.dma_start(w1[:, :, 3, :], a["L1_xattn_W_out"].rearrange("o (g c) -> o g c", c=P)).then_inc(ld["w1"], 16)
            sp.dma_start(m1_u8[:, :, :, :].rearrange("p b t k -> p (b t) k"),
                         a["mask_BxSxS2_bk1"].rearrange("b (t p) k -> p (b t) k", p=P)).then_inc(ld["m1"], 16)
            sp.dma_start(wg[:, :], a["L1_ffn_Wg"]).then_inc(ld["moe"], 16)
            for s, w, shared in ((we1, "L1_ffn_W1", "L1_ffn_Ws1"), (we3, "L1_ffn_W3", "L1_ffn_Ws3")):
                sp.dma_start(s[:, 0:PAIRS, :].rearrange("p q (e h) -> p (q e) h", h=HID),
                             a[w].rearrange("e d h -> d e h")).then_inc(ld["moe"], 16)
                sp.dma_start(s[:, PAIRS, :], a[shared]).then_inc(ld["moe"], 16)
            sp.wait_ge(job_done, NUMBER["weights", 15] + 1)
            sp.dma_start(we2[:, 0:PAIRS, :], a["L1_ffn_W2"].rearrange("(q e) h d -> (e h) q d", e=2)).then_inc(ld["moe"], 16)
            sp.dma_start(we2[:, PAIRS, :], a["L1_ffn_Ws2"]).then_inc(ld["moe"], 16)
            for b in range(B):
                sp.wait_ge(y_used, 5 + b)
                sp.dma_start(out.rearrange("b (t p) d -> p b t d", p=P)[:, b, :, :],
                             x_sb[:, NQ * b:NQ * b + NQ, :]).then_inc(stored, 16)
            sp.wait_ge(stored, 16 * B)

        @block.gpsimd
        def _(pool):
            steps, told, late = [0], [0], [0]

            def step(ins):
                steps[0] += 1
                ins.then_inc(pool_step, 1)
                pool.wait_ge(pool_step, steps[0])

            def publish(ins):
                told[0] += 1
                ins.then_inc(const_ready, 1)
                pool.wait_ge(const_ready, told[0])

            def publish_late(ins):
                late[0] += 1
                ins.then_inc(late_ready, 1)
                pool.wait_ge(late_ready, late[0])

            pool.memset(w0[:, :, 2:4, :], 0.0).then_inc(zeros_ready, 1)
            step(pool.memset(ident[:, :], 0.0))
            publish(pool.affine_select(out=ident[:, :], in_=ident[:, :], compare_op=ALU.not_equal, fill=1.0,
                                       base=0, pattern=[[-1, P]], channel_multiplier=1))
            publish(pool.memset(neg_half[:, :], -0.5))
            for q, (sign_k, sign_q) in enumerate(((0.0, 0.0), (-1.0, 0.0), (0.0, -1.0), (-1.0, -1.0))):
                rows = slice(32 * q, 32 * q + 32)
                publish(pool.memset(lo_k[rows, :], sign_k))
                publish(pool.memset(lo_q[rows, :], sign_q))
            step(pool.memset(head_row[:, :], 1.0))
            for r in range(4):
                rows = head_row[32 * r:32 * r + 32, :]
                step(pool.affine_select(out=rows, in_=rows, compare_op=ALU.is_ge, fill=0.0, base=0,
                                        pattern=[[-8, 4]], channel_multiplier=1))
                step(pool.affine_select(out=rows, in_=rows, compare_op=ALU.is_ge, fill=0.0, base=7,
                                        pattern=[[8, 4]], channel_multiplier=-1))
            pool.wait_ge(zeros_ready, 1)
            pool.wait_ge(ld["wo0"], 16)
            pool.tensor_copy(w0[:, :, 3, :].rearrange("p g (j c) -> p g j c", c=32)[:, :, :, 0:8],
                             wo0[:, :].rearrange("p (g j c) -> p g j c", j=4, c=8)).then_inc(wo0_ready, 1)
            publish_late(pool.memset(val[:, :, :, :], 0.0))
            publish_late(pool.memset(q1_high[64:P, :, 0, :].bitcast(F32), 0.0))
            publish_late(pool.memset(q1_high[0:64, :, 1, :].bitcast(F32), 0.0))

            def rstd_of(n, b):
                pool.wait_ge(var_ready, LN[n, b] + 1)
                ts = ln_tiles(n, b)
                cols = slice(ts[0], ts[-1] + 1)
                pool.tensor_tensor(rstd[:, cols], veps[:, cols], neg_half[:, cols], ALU.pow).then_inc(rstd_ready, 1)

            def norm(u):
                pool.wait_ge(recipped, u + 1)
                p = probs[:, u % NP, :]
                pool.tensor_scalar(p, p, rsum[:, u % NCOL:u % NCOL + 1], 1.0, ALU.mult, ALU.mult).then_inc(normed, 1)

            def q_stack(m):
                pool.wait_ge(stack_ready, m + 1)
                if m >= 2:
                    pool.wait_ge(scored, BLOCKS[m - 2].end)
                for j in range(4):
                    pool.tensor_scalar(q0[:, m % 2, j, :], stack_f[:, :], head_row[:, j:j + 1], 1.0,
                                       ALU.mult, ALU.mult).then_inc(q0_ready, 1)

            rstd_of(0, 0)
            pool.wait_ge(ld["m0"], 16)
            pool.tensor_scalar(mask0[:, :, :], m0_u8[:, :, :], FAR, -FAR, ALU.mult, ALU.add).then_inc(mask_ready[0], 1)
            q_stack(0)
            for t in range(-LEAD, TOTAL):
                if 0 <= t + LEAD - 3 < TOTAL:
                    norm(t + LEAD - 3)
                for job in PLAN.get(t - 1, ()):
                    if job[0] == "q" and BLOCKS[job[1]].layer == 0:
                        q_stack(job[1])
                for b in range(B):
                    if t == Y_DONE[0, b] + 1:
                        rstd_of(1, b)
                    if t == Y_DONE[0, b] + 13:
                        rstd_of(2, b)
                if t == Y_DONE[1, 0] + 1:
                    rstd_of(3, 0)
                if t == 12:
                    pool.wait_ge(ld["m1"], 16)
                    for b in range(B):
                        pool.tensor_scalar(mask1[:, b, :, :], m1_u8[:, b, :, :], -FAR, 0.0, ALU.mult,
                                           ALU.add).then_inc(mask_ready[1], 1)
                if t == TOTAL // 2 + 8:
                    pool.wait_ge(job_done, NUMBER["k", 8] + 1)
                    pool.wait_ge(normed, t + LEAD - 2)
                    step(pool.memset(spread_f[:, :, :], 0.0))
                    for half in range(2):
                        rows = spread_f[32 * half:32 * half + 32, :, :]
                        publish_late(pool.affine_select(out=rows, in_=rows, compare_op=ALU.not_equal, fill=1.0,
                                                        base=0, pattern=[[-1, EXPERTS], [0, HID]],
                                                        channel_multiplier=1))
                    publish_late(pool.memset(ones32[:, :], 1.0))
                    publish_late(pool.memset(ones_b[:, :], 1.0))
                    publish_late(pool.affine_select(out=before_b[:, :], in_=ones_b[:, :], compare_op=ALU.is_gt,
                                                    fill=0.0, base=0, pattern=[[1, P]], channel_multiplier=-1))
                    publish_late(pool.memset(gateT[64:P, :].bitcast(F32), 0.0))
            rstd_of(3, 1)

        @block.scalar
        def _(act):
            act.dma_start(wo0[:, :], a["L0_xattn_Wo"]).then_inc(ld["wo0"], 16)
            for r in range(4):
                rows = slice(32 * r, 32 * r + 32)
                act.dma_start(w0[rows, :, 0, :], a["L0_xattn_Wq"].rearrange("(g p) d -> p g d", p=32)).then_inc(ld["w0"], 16)
            act.wait_ge(zeros_ready, 1)
            for j in range(4):
                act.dma_start(w0[32 * j:32 * j + 8, :, 2, :],
                              a["L0_xattn_Wv"].rearrange("(g j p) d -> j p g d", j=4, p=8)[j]).then_inc(ld["w0"], 16)
            for r in range(4):
                rows = slice(32 * r, 32 * r + 32)
                for t, w in ((bk0, "L0_xattn_bk"), (bq0, "L0_xattn_bq")):
                    act.dma_start(t[rows, :], a[w].rearrange("(g p) -> p g", p=32),
                                  allow_slow_non_contiguous=True).then_inc(ld["b0"], 16)
            act.dma_start(bv0[:, :], a["L0_xattn_bv"].partition_broadcast(P)).then_inc(ld["bv0"], 16)
            act.dma_start(bo0[:, :], a["L0_xattn_bo"].partition_broadcast(P)).then_inc(ld["bv0"], 16)
            act.dma_start(gates[:, 0:2], a["g_xattn"].partition_broadcast(P)).then_inc(ld["g"], 16)
            act.dma_start(gates[:, 2:4], a["g_ffn"].partition_broadcast(P)).then_inc(ld["g"], 16)
            for t, w in ((bk1, "L1_xattn_b_K"), (bq1, "L1_xattn_b_Q")):
                act.dma_start(t[:, :], a[w].rearrange("(g p) -> p g", p=P),
                              allow_slow_non_contiguous=True).then_inc(ld["b1"], 16)
            act.dma_start(bv1[:, :], a["L1_xattn_b_V"].partition_broadcast(P)).then_inc(ld["bv1"], 16)
            act.dma_start(bo1[:, :], a["L1_xattn_b_out"].partition_broadcast(P)).then_inc(ld["bv1"], 16)

            def exp(u):
                act.wait_ge(maxed, u + 1)
                if u >= NP:
                    act.wait_ge(turned, u - NP + 1)
                if u >= NCOL:
                    act.wait_ge(recipped, u - NCOL + 1)
                c = u % NCOL
                act.activation(probs[:, u % NP, :], masked[:, u % NS, :], ACT.Exp, scale=-1.0,
                               bias=neg_max[:, c:c + 1], accum_out=sums[:, c:c + 1]).then_inc(exped, 1)

            def copy_turned(u):
                k, h, qt = unit(u)
                act.wait_ge(turned, u + 1)
                if k.m >= 2:
                    act.wait_ge(mixed, k.m - 1)
                act.activation(probsT[:, k.m % 2, h, :, qt * P:qt * P + P],
                               turn_bank[0][:, :].rearrange("p (k q) -> p k q", q=P), ACT.Copy).then_inc(copied_act, 1)

            def mix_copy(k):
                act.wait_ge(mixed, k.m + 1)
                if k.m >= 2:
                    act.wait_ge(projected_out, k.m - 1)
                act.activation(mixT[:, k.m % 2, :], mix_bank[:, 0:SQ], ACT.Copy).then_inc(mix_copied, 1)

            def job(j):
                name, n = j[0], NUMBER[j]
                if name in ("v", "ffn", "rank"):
                    return
                job_bank, free = job_banks[PLACE[j][0]], job_free[PLACE[j][0]]
                act.wait_ge(job_done, n + 1)
                if name == "weights":
                    k = BLOCKS[j[1]]
                    act.activation((w0T, w1T)[k.layer][:, k.g, :, :].rearrange("p a c -> p (a c)"), job_bank[:, :],
                                   ACT.Copy).then_inc(free, 1)
                elif name in ("k", "q"):
                    k = BLOCKS[j[1]]
                    cols = SK if name == "k" else SQ
                    bias = ((bq0, bk0), (bq1, bk1))[k.layer][name == "k"]
                    if k.layer == 1:
                        act.wait_ge(ld["b1"], 32)
                    full, high = ((full_q, high_q), (full_k, high_k))[name == "k"]
                    if name == "k" and k.m >= 1:
                        act.wait_ge(k_ready, k.m)
                    elif k.m >= 1:
                        act.wait_ge(*((stack_ready, k.m) if k.m <= 8 else (q1_ready, k.m - 8)))
                    act.activation(full[:, :], job_bank[:, 0:cols], ACT.Identity,
                                   bias=bias[:, k.g:k.g + 1]).then_inc(full_ready, 1)
                    if k.layer == 0:
                        act.activation(high[:, :], job_bank[:, 0:cols], ACT.Identity,
                                       bias=bias[:, k.g:k.g + 1]).then_inc(free, 1)
                    else:
                        act.wait_ge(scored, BLOCKS[k.m - 2].end)
                        act.wait_ge(late_ready, 3)
                        dst = (q1_high, k1_high)[name == "k"]
                        for h in range(2):
                            rows = slice(64 * h, 64 * h + 64)
                            ins = act.activation(dst[rows, k.m % 2, h, :], job_bank[rows, 0:cols], ACT.Identity,
                                                 bias=bias[rows, k.g:k.g + 1])
                            ins.then_inc(*((free, 1) if h == 1 else (half_done, 1)))
                elif name == "ln":
                    ts = ln_tiles(*j[1:])
                    act.activation(xnT[:, j[1] % 3, ts[0] * P:(ts[-1] + 1) * P], job_bank[:, 0:len(ts) * P],
                                   ACT.Copy).then_inc(free, 1)
                elif name == "rotate":
                    act.activation(xh[:, :, :].rearrange("p t c -> p (t c)"), job_bank[:, 0:SQ], ACT.Copy).then_inc(free, 1)
                elif name == "turn_xq":
                    act.activation(xqT[:, :], job_bank[:, 0:SQ], ACT.Copy).then_inc(free, 1)
                elif name == "logits":
                    act.wait_ge(lmax_ready, j[1] + 1)
                    for t in range(NQ):
                        ins = act.activation(ex[:, t, :], job_bank[:, t * EXPERTS:(t + 1) * EXPERTS], ACT.Exp,
                                             bias=lg[:, t:t + 1], accum_out=ls[:, t:t + 1])
                        ins.then_inc(*((free, 1) if t == NQ - 1 else (half_done, 1)))
                elif name == "turn_gate":
                    act.activation(gate_full[:, :], job_bank[0:2 * EXPERTS, 0:SQ], ACT.Copy).then_inc(gate_copied, 1)
                    act.activation(gate_hi[:, :], job_bank[0:2 * EXPERTS, 0:SQ], ACT.Copy).then_inc(free, 1)

            for i in range(2):
                act.wait_ge(ctx_turned, i + 1)
                act.activation(ctxT[:, 512 * i:512 * i + 512], turn_bank[i][:, :], ACT.Copy).then_inc(ctxT_ready, 1)
            act.wait_ge(ld["b0"], 16 * 8)
            for j in BEFORE:
                job(j)
            act.wait_ge(ld["g"], 32)
            act.activation(tanh_g[:, :], gates[:, :], ACT.Tanh).then_inc(tanh_ready, 1)
            act.wait_ge(fw_turned, 1)
            act.activation(fwT[:, :], mix_bank[:, 0:P], ACT.Copy).then_inc(fwT_ready, 1)
            for t in range(-LEAD, TOTAL + 4):
                if 0 <= t + LEAD - 2 < TOTAL:
                    exp(t + LEAD - 2)
                if 0 <= t - 1 < TOTAL and t % 2 == 1:
                    copy_turned(t - 1)
                for k in BLOCKS:
                    if t == k.end + 2:
                        mix_copy(k)
                for j in PLAN.get(t - 1, ()):
                    job(j)
            for b in range(B):
                for p in range(HALVES):
                    n = b * HALVES + p
                    act.wait_ge(u_ready, n + 1)
                    if n >= 2:
                        act.wait_ge(hid_ready, n - 1)
                    act.activation(silu[:, n % 2, :], bank[n % 2][:, 0:SQ], ACT.Silu).then_inc(silu_ready, 1)
                    if b == 0:
                        for j in AFTER.get(p - 1, ()):
                            job(j)

        @block.vector
        def _(dve):
            steps = [0]

            def step(ins):
                steps[0] += 1
                ins.then_inc(dve_step, 1)
                dve.wait_ge(dve_step, steps[0])

            def ln_stats(n, b):
                for t in ln_tiles(n, b):
                    step(dve.bn_stats(stats[:, t, :], x_sb[:, t, :]))
                    step(dve.bn_aggr(mv[:, t, :], stats[:, t, :]))
                ts = ln_tiles(n, b)
                cols = slice(ts[0], ts[-1] + 1)
                dve.tensor_scalar(veps[:, cols], mv[:, cols, 1], LN_EPS, None, ALU.add).then_inc(var_ready, 1)

            def ln_norm(n, b):
                dve.wait_ge(rstd_ready, LN[n, b] + 1)
                for t in ln_tiles(n, b):
                    dve.tensor_scalar(xn[:, t, :], x_sb[:, t, :], mv[:, t, 0:1], rstd[:, t:t + 1],
                                      ALU.subtract, ALU.mult).then_inc(xn_ready, 1)

            def add_y(layer, b, bias, gate):
                x = x_sb[:, NQ * b:NQ * b + NQ, :]
                y = y_bank[:, b * SQ:b * SQ + SQ].rearrange("p (t c) -> p t c", c=P)
                if bias is not None:
                    step(dve.tensor_tensor(tmp[:, :, :], y, bias[:, :].unsqueeze(1).to_broadcast([P, NQ, P]), ALU.add))
                    y = tmp[:, :, :]
                dve.scalar_tensor_tensor(out=x, in0=y, scalar=tanh_g[:, gate:gate + 1], in1=x,
                                         op0=ALU.mult, op1=ALU.add).then_inc(y_used, 1)
                dve.wait_ge(y_used, 2 * layer + b + 1)

            def mask_max(u):
                k, h, qt = unit(u)
                dve.wait_ge(scored, u + 1)
                if u >= NS:
                    dve.wait_ge(exped, u - NS + 1)
                mask = mask0[:, qt, :] if k.layer == 0 else mask1[:, k.b, qt, :]
                c = u % NCOL
                dve.tensor_tensor_reduce(out=masked[:, u % NS, :], in0=score_bank[u % 2][:, :], in1=mask,
                                         scale=-float(k.depth) ** -0.5, scalar=3.0e38, op0=ALU.add, op1=ALU.min,
                                         accum_out=neg_max[:, c:c + 1]).then_inc(maxed, 1)

            def recip(u):
                c = u % NCOL
                dve.wait_ge(exped, u + 1)
                if u >= NCOL:
                    dve.wait_ge(normed, u - NCOL + 1)
                dve.reciprocal(rsum[:, c:c + 1], sums[:, c:c + 1]).then_inc(recipped, 1)

            def copy_turned(u):
                k, h, qt = unit(u)
                dve.wait_ge(turned, u + 1)
                if k.m >= 2:
                    dve.wait_ge(mixed, k.m - 1)
                dve.tensor_copy(probsT[:, k.m % 2, h, :, qt * P:qt * P + P],
                                turn_bank[1][:, :].rearrange("p (k q) -> p k q", q=P)).then_inc(copied_dve, 1)

            def low_part(dst, high, whole):
                return dve.tensor_tensor(dst, whole, high.bitcast(F32), ALU.subtract)

            def job(j):
                name, n = j[0], NUMBER[j]
                job_bank, free = job_banks[PLACE[j][0]], job_free[PLACE[j][0]]
                if name == "v":
                    k = BLOCKS[j[1]]
                    dve.wait_ge(job_done, n + 1)
                    if k.m >= NV:
                        dve.wait_ge(mixed, k.m - NV + 1)
                    if k.layer == 0:
                        dst = val[:, k.m % NV, :, :].rearrange("p k (j c) -> p k j c", c=32)[:, :, :, 0:8]
                        src = job_bank[:, :].rearrange("p (k j c) -> p k j c", j=4, c=32)[:, :, :, 0:8]
                        bias = bv0[:, 32 * k.g:32 * k.g + 32].rearrange("p (j c) -> p j c", c=8).unsqueeze(1)\
                            .to_broadcast([P, NK, 4, 8])
                    else:
                        dve.wait_ge(ld["bv1"], 32)
                        dst = val[:, k.m % NV, :, :]
                        src = job_bank[:, :].rearrange("p (k c) -> p k c", c=P)
                        bias = bv1[:, P * k.g:P * k.g + P].unsqueeze(1).to_broadcast([P, NK, P])
                    dve.tensor_tensor(dst, src, bias, ALU.add).then_inc(free, 1)
                elif name in ("k", "q"):
                    k = BLOCKS[j[1]]
                    dve.wait_ge(*freed(j))
                    i = k.m % 2
                    full, high = ((full_q, high_q), (full_k, high_k))[name == "k"]
                    if k.layer == 0:
                        if name == "k":
                            if k.m >= 2:
                                dve.wait_ge(scored, BLOCKS[k.m - 2].end)
                            dst, sign, ready = k0[:, i, :], lo_k, k_ready
                        else:
                            if k.m >= 1:
                                dve.wait_ge(q0_ready, 4 * k.m)
                            dst, sign, ready = stack_f[:, :], lo_q, stack_ready
                        dve.scalar_tensor_tensor(out=dst, in0=high[:, :].bitcast(F32), scalar=sign[:, 0:1],
                                                 in1=full[:, :], op0=ALU.mult, op1=ALU.add).then_inc(ready, 1)
                        return
                    own = [slice(64 * h, 64 * h + 64) for h in range(2)]
                    if name == "k":
                        dve.wait_ge(scored, BLOCKS[k.m - 2].end)
                        for h in range(2):
                            dve.tensor_copy(k1_high[own[1 - h], i, h, :], k1_high[own[h], i, h, :]).then_inc(half_dve, 1)
                        for h in range(2):
                            ins = low_part(k1_low[own[h], i, :], k1_high[own[h], i, h, :], full[own[h], :])
                            ins.then_inc(*((k_ready, 1) if h == 1 else (half_dve, 1)))
                    else:
                        for h in range(2):
                            dve.tensor_copy(q1_both[own[h], i, h, :], q1_high[own[h], i, h, :]).then_inc(half_dve, 1)
                        for h in range(2):
                            ins = low_part(q1_both[own[1 - h], i, h, :], q1_high[own[h], i, h, :], full[own[h], :])
                            ins.then_inc(*((q1_ready, 1) if h == 1 else (half_dve, 1)))

            def quantise(b):
                dve.wait_ge(*freed(("rotate", b)))
                step(dve.tensor_reduce(qs[:, 0, :], xh[:, :, :], X, ALU.max, apply_absolute_value=True))
                step(dve.tensor_scalar(qs[:, 1, :], qs[:, 0, :], 1e-5, 1.0 / 7.0, ALU.max, ALU.mult))
                step(dve.reciprocal(qs[:, 2, :], qs[:, 1, :]))
                inv = qs[:, 2, :].unsqueeze(2).to_broadcast([P, NQ, P])
                scl = qs[:, 1, :].unsqueeze(2).to_broadcast([P, NQ, P])
                rounder = 1.5 * 2.0 ** 23
                step(dve.tensor_tensor(tmp[:, :, :], xh[:, :, :], inv, ALU.mult))
                step(dve.tensor_scalar(tmp[:, :, :], tmp[:, :, :], rounder, -rounder, ALU.add, ALU.add))
                step(dve.tensor_scalar(tmp[:, :, :], tmp[:, :, :], -8.0, 7.0, ALU.max, ALU.min))
                step(dve.tensor_tensor(tmp[:, :, :], tmp[:, :, :], scl, ALU.mult))
                step(dve.tensor_tensor(tmp[:, :, :], tmp[:, :, :], xh[:, :, :], ALU.subtract))
                dve.tensor_tensor(xq[:, :, :], xh[:, :, :], tmp[:, :, :], ALU.add).then_inc(xq_ready, 1)

            def feed_forward(b, o):
                if o == 0:
                    dve.wait_ge(projected_out, 4 * b + 4)
                    dve.wait_ge(tanh_ready, 1)
                    add_y(0, b, bo0, 0)
                    ln_stats(1, b)
                if o == 2:
                    ln_norm(1, b)
                if o == 7:
                    quantise(b)
                if o == 12:
                    j = ("ffn", b)
                    n = NUMBER[j]
                    job_bank, free = job_banks[PLACE[j][0]], job_free[PLACE[j][0]]
                    dve.wait_ge(job_done, n + 1)
                    x = x_sb[:, NQ * b:NQ * b + NQ, :]
                    dve.scalar_tensor_tensor(out=x, in0=job_bank[:, 0:SQ].rearrange("p (t c) -> p t c", c=P),
                                             scalar=tanh_g[:, 2:3], in1=x, op0=ALU.mult, op1=ALU.add).then_inc(free, 1)
                    dve.wait_ge(*freed(("ffn", b)))
                    ln_stats(2, b)
                if o == 14:
                    ln_norm(2, b)

            def router(b, o):
                if o == 0:
                    dve.wait_ge(projected_out, 8 + 8 * b + 8)
                    add_y(1, b, bo1, 1)
                    ln_stats(3, b)
                if o == 2:
                    ln_norm(3, b)
                if o == (6, 5)[b]:
                    dve.wait_ge(job_done, NUMBER["logits", b] + 1)
                    job_bank = job_banks[PLACE["logits", b][0]]
                    logits = job_bank[:, 0:NQ * EXPERTS].rearrange("p (t e) -> p t e", e=EXPERTS)
                    dve.tensor_reduce(lg[:, :], logits, X, ALU.max, negate=True).then_inc(lmax_ready, 1)
                if o == 7:
                    dve.wait_ge(late_ready, 9)
                    dve.wait_ge(*freed(("logits", b)))
                    step(dve.reciprocal(lr[:, :], ls[:, :]))
                    step(dve.tensor_tensor(sc[:, :, :], ex[:, :, :], lr[:, :].unsqueeze(2).to_broadcast([P, NQ, EXPERTS]), ALU.mult))
                    for t in range(NQ):
                        step(dve.max(top8[:, t, :], sc[:, t, :]))
                    fourth = top8[:, :, TOP - 1:TOP].to_broadcast([P, NQ, EXPERTS])
                    step(dve.tensor_tensor(above[:, :, :], sc[:, :, :], fourth, ALU.is_gt))
                    step(dve.tensor_tensor(equal[:, :, :], sc[:, :, :], fourth, ALU.is_equal))
                    step(dve.tensor_reduce(lg[:, :], above[:, :, :], X, ALU.add))
                    step(dve.tensor_scalar(room[:, :], lg[:, :], -1.0, float(TOP), ALU.mult, ALU.add))
                    for t in range(NQ):
                        step(dve.tensor_tensor_scan(run[:, t, :], ones32[:, :], equal[:, t, :], 0.0, ALU.mult, ALU.add))
                    step(dve.tensor_tensor(run[:, :, :], run[:, :, :], room[:, :].unsqueeze(2).to_broadcast([P, NQ, EXPERTS]), ALU.is_le))
                    step(dve.tensor_tensor(run[:, :, :], run[:, :, :], equal[:, :, :], ALU.mult))
                    step(dve.tensor_tensor(sel[:, :, :], run[:, :, :], above[:, :, :], ALU.add))
                    dve.tensor_copy(sel_b[:, NQ * b:NQ * b + NQ, :], sel[:, :, :]).then_inc(sel_ready, 1)
                if o == 10:
                    j = ("rank", b)
                    n = NUMBER[j]
                    job_bank, free = job_banks[PLACE[j][0]], job_free[PLACE[j][0]]
                    dve.wait_ge(job_done, n + 1)
                    rank = job_bank[:, 0:NQ * EXPERTS].rearrange("p (t e) -> p t e", e=EXPERTS)
                    dve.scalar_tensor_tensor(out=kept[:, :, :], in0=rank, scalar=float(CAP), in1=sel[:, :, :],
                                             op0=ALU.is_lt, op1=ALU.mult).then_inc(free, 1)
                    dve.wait_ge(*freed(("rank", b)))
                    for i in range(2):
                        dve.tensor_tensor(wgt[:, :, i, :], kept[:, :, :], sc[:, :, :], ALU.mult).then_inc(wgt_ready, 1)
                if o == 12:
                    dve.wait_ge(*freed(("turn_gate", b)))
                    dve.scalar_tensor_tensor(out=gateT[0:2 * EXPERTS, b * SQ:b * SQ + SQ], in0=gate_hi[:, :].bitcast(F32),
                                             scalar=lo_k[0:2 * EXPERTS, 0:1], in1=gate_full[:, :],
                                             op0=ALU.mult, op1=ALU.add).then_inc(gateT_ready, 1)

            dve.wait_ge(ld["x"], 16)
            ln_stats(0, 0)
            ln_norm(0, 0)
            dve.wait_ge(const_ready, 10)
            dve.wait_ge(late_ready, 1)
            dve.wait_ge(ld["bv0"], 32)
            for j in BEFORE:
                job(j)
            dve.wait_ge(ld["fw"], 16)
            step(dve.tensor_reduce(fcol[:, 0:1], fw[:, :], X, ALU.add, apply_absolute_value=True))
            step(dve.tensor_scalar(fcol[:, 1:2], fcol[:, 0:1], 1.0 / P, 1e-5, ALU.mult, ALU.max))
            step(dve.reciprocal(fcol[:, 2:3], fcol[:, 1:2]))
            step(dve.tensor_scalar(fq[:, :], fw[:, :], fcol[:, 2:3], None, ALU.mult))
            step(dve.tensor_scalar(fs[:, 0, :], fq[:, :], 0.5, None, ALU.is_gt))
            step(dve.tensor_scalar(fs[:, 1, :], fq[:, :], -0.5, None, ALU.is_lt))
            step(dve.tensor_tensor(fs[:, 0, :], fs[:, 0, :], fs[:, 1, :], ALU.subtract))
            step(dve.scalar_tensor_tensor(out=fs[:, 1, :], in0=fs[:, 0, :], scalar=fcol[:, 1:2], in1=fw[:, :],
                                          op0=ALU.mult, op1=ALU.subtract))
            dve.tensor_tensor(fq[:, :], fw[:, :], fs[:, 1, :], ALU.add).then_inc(fw_ready, 1)
            dve.wait_ge(mask_ready[0], 1)
            for t in range(-LEAD, TOTAL + 4):
                if t + LEAD - 1 == TOTAL // 2:
                    dve.wait_ge(mask_ready[1], 2)
                if 0 <= t + LEAD - 1 < TOTAL:
                    mask_max(t + LEAD - 1)
                if 0 <= t + LEAD - 3 < TOTAL:
                    recip(t + LEAD - 3)
                if 0 <= t - 1 < TOTAL and t % 2 == 0:
                    copy_turned(t - 1)
                for b in range(B):
                    feed_forward(b, t - Y_DONE[0, b])
                router(0, t - Y_DONE[1, 0])
                for j in PLAN.get(t - 1, ()):
                    job(j)
                if t == Y_DONE[1, 0] - 4:
                    dve.wait_ge(late_ready, 5)
                    dve.tensor_copy(spread[:, :, :], spread_f[:, :, :]).then_inc(spread_ready, 1)
            for b in range(B):
                for p in range(HALVES):
                    n = b * HALVES + p
                    i = n % 2
                    if b == 0 and p == 0:
                        router(1, 0)
                    dve.wait_ge(silu_ready, n + 1)
                    dve.wait_ge(v_ready, n + 1)
                    if n >= 2:
                        dve.wait_ge(down_done, n - 1)
                    if p < PAIRS:
                        dve.tensor_tensor(prod[:, i, :], bank[2 + i][:, 0:SQ], silu[:, i, :], ALU.mult).then_inc(prod_ready, 1)
                        dve.wait_ge(g_ready, b * PAIRS + p + 1)
                        dve.wait_ge(prod_ready, b * PAIRS + p + 1)
                        dve.tensor_tensor(hidT[:, i, :], bank[4 + i][:, 0:SQ], prod[:, i, :], ALU.mult).then_inc(hid_ready, 1)
                    else:
                        dve.tensor_tensor(hidT[:, i, :], bank[2 + i][:, 0:SQ], silu[:, i, :], ALU.mult).then_inc(hid_ready, 1)
                    if b == 0 and p > 0:
                        router(1, p)
                dve.wait_ge(down_done, (b + 1) * HALVES)
                add_y(2, b, None, 3)

        @block.tensor
        def _(pe):
            def turn_tiles(dst, tiles, rows=P):
                for t, src in enumerate(tiles):
                    ins = pe.transpose(dst[0:rows, t * P:t * P + P], src, ident[:, :])
                return ins

            def job(j):
                name, (i, before) = j[0], PLACE[j]
                job_bank = job_banks[i]
                if before:
                    pe.wait_ge(job_free[i], before)
                if name in ("weights", "k", "q", "v"):
                    k = BLOCKS[j[1]]
                    wT = (w0T, w1T)[k.layer][:, k.g, :, :]
                    if name != "weights":
                        pe.wait_ge(*freed(("weights", k.m - k.b * k.groups)))
                    if name == "weights":
                        if k.layer == 1 and k.g == 0:
                            pe.wait_ge(ld["w1"], 64)
                        w = (w0, w1)[k.layer]
                        ins = turn_tiles(job_bank, [w[:, k.g, i, :] for i in range(4)])
                    elif name == "q":
                        pe.wait_ge(*freed(("ln", 2 * k.layer, k.b * k.layer)))
                        ins = pe.matmul(job_bank[:, 0:SQ], wT[:, 0, :], xnT[:, 2 * k.layer, k.b * SQ:k.b * SQ + SQ],
                                        start=True, stop=True)
                    elif name == "k":
                        ins = pe.matmul(job_bank[:, :], wT[:, 1, :], ctxT[:, k.b * SK:k.b * SK + SK], start=True, stop=True)
                    else:
                        for i in range(NK):
                            c = (k.b * NK + i) * P
                            ins = pe.matmul(job_bank[:, i * P:i * P + P], ctxT[:, c:c + P], wT[:, 2, :], start=True, stop=True)
                elif name == "ln":
                    pe.wait_ge(xn_ready, xn_count(*j[1:]))
                    ins = turn_tiles(job_bank, [xn[:, t, :] for t in ln_tiles(*j[1:])])
                elif name == "rotate":
                    pe.wait_ge(ld["had"], 16)
                    pe.wait_ge(*freed(("ln", 1, j[1])))
                    b = j[1]
                    for t in range(NQ):
                        c = b * SQ + t * P
                        ins = pe.matmul(job_bank[:, t * P:t * P + P], xnT[:, 1, c:c + P], had[:, :], start=True, stop=True)
                elif name == "turn_xq":
                    pe.wait_ge(xq_ready, j[1] + 1)
                    ins = turn_tiles(job_bank, [xq[:, t, :] for t in range(NQ)])
                elif name == "ffn":
                    pe.wait_ge(fwT_ready, 1)
                    pe.wait_ge(*freed(("turn_xq", j[1])))
                    for t in range(NQ):
                        ins = pe.matmul(job_bank[:, t * P:t * P + P], xqT[:, t * P:t * P + P], fwT[:, :], start=True, stop=True)
                elif name == "logits":
                    pe.wait_ge(ld["moe"], 16 * 7)
                    pe.wait_ge(*freed(("ln", 3, j[1])))
                    for t in range(NQ):
                        c = j[1] * SQ + t * P
                        ins = pe.matmul(job_bank[:, t * EXPERTS:(t + 1) * EXPERTS], xnT[:, 0, c:c + P], wg[:, :],
                                        start=True, stop=True)
                elif name == "rank":
                    pe.wait_ge(sel_ready, j[1] + 1)
                    for i in range(NQ):
                        t = j[1] * NQ + i
                        for s in range(t + 1):
                            ins = pe.matmul(job_bank[:, i * EXPERTS:(i + 1) * EXPERTS],
                                            (before_b if s == t else ones_b)[:, :], sel_b[:, s, :],
                                            start=(s == 0), stop=(s == t))
                else:
                    pe.wait_ge(wgt_ready, 2 * j[1] + 2)
                    ins = turn_tiles(job_bank, [wgt[:, t, :, :].rearrange("p a e -> p (a e)") for t in range(NQ)],
                                     rows=2 * EXPERTS)
                ins.then_inc(job_done, 1)

            def scores(u):
                k, h, qt = unit(u)
                dst = score_bank[u % 2][:, :]
                i, q = k.m % 2, slice(qt * P, qt * P + P)
                pe.wait_ge(k_ready, k.m + 1)
                if u >= 2:
                    pe.wait_ge(maxed, u - 1)
                if k.layer == 0:
                    pe.wait_ge(q0_ready, 4 * k.m + h + 1)
                    pe.matmul(dst, q0[:, i, h, q], k0[:, i, :], start=True, stop=True).then_inc(scored, 1)
                else:
                    pe.wait_ge(q1_ready, k.m - 7)
                    pe.matmul(dst, q1_both[:, i, h, q], k1_high[:, i, h, :], start=True, stop=False)
                    pe.matmul(dst, q1_high[:, i, h, q], k1_low[:, i, :], start=False, stop=True).then_inc(scored, 1)

            def turn(u):
                pe.wait_ge(normed, u + 1)
                if u >= 2:
                    pe.wait_ge(copied_dve if u % 2 else copied_act, u // 2)
                turn_tiles(turn_bank[u % 2], [probs[:, u % NP, i * P:i * P + P] for i in range(NK)]).then_inc(turned, 1)

            def mix(k):
                pe.wait_ge(copied_act, k.end // 2)
                pe.wait_ge(copied_dve, k.end // 2)
                pe.wait_ge(*freed(("v", k.m)))
                if k.m >= 1:
                    pe.wait_ge(mix_copied, k.m)
                w = k.width
                for i in range(NK):
                    for h in range(k.heads):
                        ins = pe.matmul(mix_bank[w * h:w * h + w, 0:SQ], val[:, k.m % NV, i, w * h:w * h + w],
                                        probsT[:, k.m % 2, h, i, :], start=(i == 0), stop=(i == NK - 1))
                ins.then_inc(mixed, 1)

            def project_out(k):
                pe.wait_ge(mix_copied, k.m + 1)
                if k.g == 0 and (k.layer or k.b):
                    pe.wait_ge(y_used, 2 * k.layer + k.b)
                for t in range(NQ):
                    c = k.b * SQ + t * P
                    ins = pe.matmul(y_bank[:, c:c + P], mixT[:, k.m % 2, t * P:t * P + P],
                                    (w0T, w1T)[k.layer][:, k.g, 3, :], start=(k.g == 0 and t == 0),
                                    stop=(k.g == k.groups - 1), skip_group_check=True)
                ins.then_inc(projected_out, 1)

            pe.wait_ge(const_ready, 1)
            for i in range(2):
                pe.wait_ge(ld[f"ctx{i}"], 16)
                turn_tiles(turn_bank[i], [ctx_sb[:, 4 * i + t, :] for t in range(4)]).then_inc(ctx_turned, 1)
            pe.wait_ge(ld["w0"], 16 * 12)
            pe.wait_ge(wo0_ready, 1)
            for n, j in enumerate(BEFORE):
                job(j)
                if n == 0:
                    pe.wait_ge(ctxT_ready, 2)
            pe.wait_ge(fw_ready, 1)
            pe.transpose(mix_bank[:, 0:P], fq[:, :], ident[:, :]).then_inc(fw_turned, 1)
            pe.wait_ge(fwT_ready, 1)
            for t in range(-LEAD, TOTAL + 4):
                if 0 <= t + LEAD < TOTAL:
                    scores(t + LEAD)
                for j in PLAN.get(t, ()):
                    job(j)
                if 0 <= t < TOTAL:
                    turn(t)
                for k in BLOCKS:
                    if t == k.end + 1:
                        mix(k)
                    if t == k.end + 3:
                        project_out(k)

            def down(n):
                b, p = divmod(n, HALVES)
                pe.wait_ge(hid_ready, n + 1)
                if p == 0:
                    pe.wait_ge(y_used, 4 + b)
                for t in range(NQ):
                    c = b * SQ + t * P
                    ins = pe.matmul(y_bank[:, c:c + P], hidT[:, n % 2, t * P:t * P + P], we2[:, p, :],
                                    start=(p == 0 and t == 0), stop=(p == PAIRS), skip_group_check=True)
                ins.then_inc(down_done, 1)

            pe.wait_ge(spread_ready, 1)
            for b in range(B):
                pe.wait_ge(gateT_ready, b + 1)
                xT = xnT[:, 0, b * SQ:b * SQ + SQ]
                for p in range(HALVES):
                    n = b * HALVES + p
                    i = n % 2
                    if n >= 2:
                        pe.wait_ge(silu_ready, n - 1)
                    pe.matmul(bank[i][:, 0:SQ], we1[:, p, :], xT, start=True, stop=True).then_inc(u_ready, 1)
                    if n >= 2:
                        pe.wait_ge(hid_ready, n - 1)
                    pe.matmul(bank[2 + i][:, 0:SQ], we3[:, p, :], xT, start=True, stop=True).then_inc(v_ready, 1)
                    if p < PAIRS:
                        pe.matmul(bank[4 + i][:, 0:SQ], spread[:, 2 * p:2 * p + 2, :].rearrange("p e h -> p (e h)"),
                                  gateT[:, b * SQ:b * SQ + SQ], start=True, stop=True).then_inc(g_ready, 1)
                    if n >= 1:
                        down(n - 1)
                    if b == 0:
                        for j in AFTER.get(p, ()):
                            job(j)
            down(B * HALVES - 1)


_INS = ["x", "ctx_1024", "mask_1x1xSxS2_bk0", "mask_BxSxS2_bk1", "g_xattn", "g_ffn", "L0_xattn_Wq", "L0_xattn_bq",
        "L0_xattn_Wk", "L0_xattn_bk", "L0_xattn_Wv", "L0_xattn_bv", "L0_xattn_Wo", "L0_xattn_bo", "L0_ffn_weight",
        "L1_xattn_W_Q", "L1_xattn_b_Q", "L1_xattn_W_K", "L1_xattn_b_K", "L1_xattn_W_V", "L1_xattn_b_V",
        "L1_xattn_W_out", "L1_xattn_b_out", "L1_ffn_Wg", "L1_ffn_W1", "L1_ffn_W2", "L1_ffn_W3", "L1_ffn_Ws1",
        "L1_ffn_Ws2", "L1_ffn_Ws3"]


def kernel(**inputs):
    import numpy as _np
    import concourse.bacc as _bacc
    from concourse import mybir as _mybir
    from concourse.bass_utils import run_bass_kernel_spmd as _run

    nc = _bacc.Bacc("TRN2", target_bir_lowering=False, num_devices=1)
    arrays, args = {}, {}

    def give(name, array):
        arrays[f"in_{name}"] = array
        args[name] = nc.dram_tensor(f"in_{name}", array.shape, _mybir.dt.from_np(array.dtype), kind="ExternalInput").ap()

    for name in _INS:
        give(name, _np.ascontiguousarray(inputs[name]))
    had = _np.array([[1.0]])
    while had.shape[0] < 128:
        had = _np.block([[had, had], [had, -had]])
    give("hadamard", (had / _np.sqrt(128)).astype(_np.float32))
    out = nc.dram_tensor("out_0", (2, 256, 128), _mybir.dt.float32, kind="ExternalOutput").ap()
    build(nc, args, out)
    r = _run(nc, [arrays], core_ids=[0])
    return r.results[0]["out_0"]
```

```python
import concourse.bass as bass
from concourse import mybir
from contextlib import ExitStack

F32 = mybir.dt.float32
F32R = mybir.dt.float32r
BF16 = mybir.dt.bfloat16
U8 = mybir.dt.uint8
ALU = mybir.AluOpType
ACT = mybir.ActivationFunctionType
X = mybir.AxisListType.X

P = 128
B, SQ, SK = 2, 256, 512
TOK = B * SQ
NT = TOK // P
NC = B * SK // P
NQ = SQ // P
NK = SK // P
LN_EPS = 1e-5
FAR = 1.7e38
EXPERTS, HID, TOP = 32, 64, 4
CAP = 4 * TOK * TOP // EXPERTS
PAIRS = EXPERTS // 2
HALVES = PAIRS + 1

LEAD = 6
NS, NP, NCOL = 3, 6, 8
NV = 4


class Block:

    def __init__(self, m, layer, b, g, first):
        self.m, self.layer, self.b, self.g, self.first = m, layer, b, g, first
        self.heads, self.width, self.depth = ((4, 32, 8), (2, 64, 64))[layer]
        self.groups = (4, 8)[layer]
        self.units = self.heads * NQ
        self.end = first + self.units
        last = layer == 1 and b == B - 1 and g == self.groups - 1
        self.mix_at = (self.end + 1, self.end + (1 if last else (2, 3)[layer]))
        self.copy_at = self.mix_at[1] + (2 if layer == 1 and not last else 1)
        self.out_at = self.copy_at + 1


def make_blocks():
    blocks, first = [], 0
    for layer in range(2):
        for b in range(B):
            for g in range((4, 8)[layer]):
                blocks.append(Block(len(blocks), layer, b, g, first))
                first = blocks[-1].end
    return blocks


BLOCKS = make_blocks()
TOTAL = BLOCKS[-1].end
EXPERTS_AT = TOTAL + 2
Y_DONE = {(k.layer, k.b): k.out_at + 1 for k in BLOCKS if k.g == k.groups - 1}


def make_plan():
    before = [("weights", 0), ("k", 0), ("ln", 0, 0), ("q", 0), ("v", 0), ("weights", 1)]
    plan = {}
    ahead = ({"weights": 17, "k": 13, "q": 11, "v": 10}, {"k": 11, "q": 9, "v": 4})
    for k in BLOCKS[1:]:
        if k.layer == 1 and k.b == 0:
            plan.setdefault(BLOCKS[k.g].first, []).append(("weights", k.m))
        for name, slots in ahead[k.layer].items():
            if name != "weights" or (k.b == 0 and k.m > 1):
                plan.setdefault(k.first - slots, []).append((name, k.m))
    plan.setdefault(4, []).append(("turn_fw",))
    for b in range(B):
        for o, job in ((4, ("ln", 1, b)), (7, ("rotate", b)), (11, ("turn_xq", b)), (13, ("ffn", b)),
                       (17, ("ln", 2, b))):
            plan.setdefault(Y_DONE[0, b] + o, []).append(job)
    after = {}
    for o, name in ((4, "ln"), (6, "logits"), (11, "rank"), (13, "turn_gate")):
        for b in range(B):
            job = (name, 3, b) if name == "ln" else (name, b)
            (after if b else plan).setdefault(Y_DONE[1, b] + o, []).append(job)
    order = before + [j for t in sorted(plan) for j in plan[t]] + [j for o in sorted(after) for j in after[o]]
    number = {j: n for n, j in enumerate(order)}
    last = [j for o in after for j in after[o]]
    place, count = {}, [0, 0]
    for j in order:
        i = 1 if j in last else number[j] % 2
        place[j] = (i, count[i])
        count[i] += 1
    highs, count = {}, 0
    for j in order:
        if j[0] in ("k", "q"):
            count += 2 if j[0] == "q" and BLOCKS[j[1]].layer == 1 else 1
            highs[j] = count
    return before, plan, after, number, place, highs


BEFORE, PLAN, AFTER, NUMBER, PLACE, HIGHS = make_plan()

MORE_ON_ACT = (36, 46, 48, 68, 70, 78, 80, 102, 110, 112)
SPREAD_STEP = 8
SPREAD_AT = [BLOCKS[12].first + 1 + 4 * i for i in range(EXPERTS // SPREAD_STEP)]


def on_act(u):
    return u % 2 == 1 or u in MORE_ON_ACT


def unit(u):
    k = [k for k in BLOCKS if k.first <= u < k.end][0]
    return (k, *divmod(u - k.first, NQ))


def build(nc, a, out):
    ctx = ExitStack()
    with ctx:
        def sb(name, shape, dt=F32):
            return ctx.enter_context(nc.sbuf_tensor(name, shape, dt))

        def sem(name):
            return ctx.enter_context(nc.semaphore(name))

        bank = [ctx.enter_context(nc.psum_tensor(f"bank{i}", [P, 512], F32)) for i in range(8)]
        score_bank = bank[0:2]
        turn_bank = bank[2:4]
        mix_bank, y_bank = bank[4], bank[7]
        job_banks = bank[5:7]
        u_bank, v_bank, g_bank, moe_bank = bank[0:2], bank[2:4], bank[5], (bank[4], bank[7])

        ident = sb("ident", [P, P])
        had = sb("had", [P, P])
        lo_k = sb("lo_k", [P, 1])
        lo_q = sb("lo_q", [P, 1])
        head_row = sb("head_row", [P, 4])
        gates = sb("gates", [P, 4])
        tanh_g = sb("tanh_g", [P, 4])
        x_sb = sb("x_sb", [P, NT, P])
        ctx_sb = sb("ctx_sb", [P, NC, P])
        ctxT = sb("ctxT", [P, NC * P])

        xn = sb("xn", [P, NT, P])
        xnT = sb("xnT", [P, 3, TOK])
        stats = sb("stats", [P, NT, 6])
        mv = sb("mv", [P, NT, 2])
        veps = sb("veps", [P, NT])
        neg_half = sb("neg_half", [P, NT])
        rstd = sb("rstd", [P, NT])
        tmp = sb("tmp", [P, NQ, P])

        masked = sb("masked", [P, NS, SK])
        probs = sb("probs", [P, NP, SK])
        neg_max = sb("neg_max", [P, NCOL])
        sums = sb("sums", [P, NCOL])
        rsum = sb("rsum", [P, NCOL])
        probsT = sb("probsT", [P, 2, 4, NK, SQ])
        mixT = sb("mixT", [P, 2, SQ])
        val = sb("val", [P, NV, NK, P])
        high_k = sb("high_k", [P, SK], F32R)
        high_q = sb("high_q", [P, SQ], F32R)
        stack_f = sb("stack_f", [P, SQ])

        w0 = sb("w0", [P, 4, 4, P])
        w0T = sb("w0T", [P, 4, 4, P])
        wo0 = sb("wo0", [P, P])
        bq0 = sb("bq0", [P, 4])
        bk0 = sb("bk0", [P, 4])
        minus_bq0 = sb("minus_bq0", [P, 4])
        minus_bk0 = sb("minus_bk0", [P, 4])
        bv0 = sb("bv0", [P, P])
        bo0 = sb("bo0", [P, P])
        m0_u8 = sb("m0_u8", [P, NQ, SK], U8)
        mask0 = sb("mask0", [P, NQ, SK], BF16)
        k0 = sb("k0", [P, 2, SK], F32R)
        q0 = sb("q0", [P, 2, 4, SQ], F32R)
        w1 = sb("w1", [P, 8, 4, P])
        w1T = sb("w1T", [P, 8, 4, P])
        bq1 = sb("bq1", [P, 8])
        bk1 = sb("bk1", [P, 8])
        bv1 = sb("bv1", [P, 8 * P])
        bo1 = sb("bo1", [P, P])
        m1_u8 = sb("m1_u8", [P, B, NQ, SK], U8)
        mask1 = sb("mask1", [P, B, NQ, SK], BF16)
        k1_high = sb("k1_high", [P, 2, SK], F32R)
        k1_both = sb("k1_both", [P, 2, 2, SK], F32R)
        q1_both = sb("q1_both", [P, 2, 2, SQ], F32R)
        q1_high = sb("q1_high", [P, 2, 2, SQ], F32R)
        fw = sb("fw", [P, P])
        fq = sb("fq", [P, P])
        fs = sb("fs", [P, 2, P])
        fcol = sb("fcol", [P, 4])
        fwT = sb("fwT", [P, P])
        xh = sb("xh", [P, NQ, P])
        xq = sb("xq", [P, NQ, P])
        xqT = sb("xqT", [P, SQ])
        qs = sb("qs", [P, 3, NQ])
        wg = sb("wg", [P, EXPERTS])
        we1 = sb("we1", [P, HALVES, P])
        we3 = sb("we3", [P, HALVES, P])
        lg = sb("lg", [P, NQ])
        ls = sb("ls", [P, NQ])
        lr = sb("lr", [P, NQ])
        ex = sb("ex", [P, NQ, EXPERTS])
        sc = sb("sc", [P, NQ, EXPERTS])
        top8 = sb("top8", [P, NQ, 8])
        above = sb("above", [P, NQ, EXPERTS])
        equal = sb("equal", [P, NQ, EXPERTS])
        run = sb("run", [P, NQ, EXPERTS])
        room = sb("room", [P, NQ])
        sel = sb("sel", [P, NQ, EXPERTS])
        sel_b = sb("sel_b", [P, NT, EXPERTS], BF16)
        kept = sb("kept", [P, NQ, EXPERTS])
        wgt = sb("wgt", [P, NQ, 2, EXPERTS])
        ones32 = sb("ones32", [P, EXPERTS])
        ones_b = sb("ones_b", [P, P], BF16)
        before_b = sb("before_b", [P, P], BF16)
        gate_hi = sb("gate_hi", [2 * EXPERTS, SQ], F32R)
        gate_full = sb("gate_full", [2 * EXPERTS, SQ])
        spread = q0[:, :, :, :].rearrange("p i h t -> p (i h t)").rearrange("p (e h) -> p e h", h=HID)
        gateT = k0[:, 0, :]
        we2 = w1[:, :, :, :].rearrange("p g a c -> p (g a) c")[:, 0:HALVES, :]
        flat = probsT[:, :, :, :, :].rearrange("p a h k q -> p (a h k q)")
        silu, prod, hidT = (flat[:, 2 * SQ * i:2 * SQ * (i + 1)].rearrange("p (i t) -> p i t", i=2) for i in range(3))

        ld = {n: sem("ld_" + n) for n in (
            "x", "ctx0", "ctx1", "g", "had", "w0", "wo0", "b0", "bv0", "m0", "w1", "b1", "bv1", "m1", "fw", "moe")}
        zeros_ready = sem("zeros_ready")
        const_ready = sem("const_ready")
        pool_step = sem("pool_step")
        wo0_ready = sem("wo0_ready")
        late_ready = sem("late_ready")
        mask_ready = [sem("mask0_ready"), sem("mask1_ready")]
        tanh_ready = sem("tanh_ready")
        ctx_turned = sem("ctx_turned")
        ctxT_ready = sem("ctxT_ready")
        fw_ready = sem("fw_ready")
        dve_step = sem("dve_step")
        var_ready = sem("var_ready")
        rstd_ready = sem("rstd_ready")
        minus_ready = sem("minus_ready")
        xn_ready = sem("xn_ready")
        scored = sem("scored")
        maxed = sem("maxed")
        exped = sem("exped")
        recipped = sem("recipped")
        normed = sem("normed")
        turned = sem("turned")
        copied = [sem("copied0"), sem("copied1")]
        mixed = sem("mixed")
        mix_copied = sem("mix_copied")
        projected_out = sem("projected_out")
        job_done = sem("job_done")
        job_free = [sem("job_free0"), sem("job_free1")]
        half_done = sem("half_done")
        half_dve = sem("half_dve")
        high_ready = sem("high_ready")
        cross_ready = sem("cross_ready")
        own_ready = sem("own_ready")
        q0_ready = sem("q0_ready")
        y_used = sem("y_used")
        xq_ready = sem("xq_ready")
        lmax_ready = sem("lmax_ready")
        sel_ready = sem("sel_ready")
        spread_ready = sem("spread_ready")
        wgt_ready = sem("wgt_ready")
        gate_copied = sem("gate_copied")
        gateT_ready = sem("gateT_ready")
        u_ready = sem("u_ready")
        v_ready = sem("v_ready")
        g_ready = sem("g_ready")
        silu_ready = sem("silu_ready")
        prod_ready = sem("prod_ready")
        hid_ready = sem("hid_ready")
        down_done = sem("down_done")
        stored = sem("stored")

        LN = {(0, 0): 0, (1, 0): 1, (2, 0): 2, (1, 1): 3, (2, 1): 4, (3, 0): 5, (3, 1): 6}

        def ln_tiles(n, b):
            return range(NT) if n == 0 else range(NQ * b, NQ * b + NQ)

        def xn_count(n, b):
            return NT + NQ * LN[n, b]

        def freed(job):
            return job_free[PLACE[job][0]], PLACE[job][1] + 1

        block = ctx.enter_context(nc.Block())

        @block.sync
        def _(sp):
            ctx_t = a["ctx_1024"].rearrange("b (t p) d -> p (b t) d", p=P)
            for r in range(4):
                sp.dma_start(w0[32 * r:32 * r + 32, :, 1, :],
                             a["L0_xattn_Wk"].rearrange("(g p) d -> p g d", p=32)).then_inc(ld["w0"], 16)
            sp.dma_start(ctx_sb[:, 0:4, :], ctx_t[:, 0:4, :]).then_inc(ld["ctx0"], 16)
            sp.dma_start(x_sb[:, :, :], a["x"].rearrange("b (t p) d -> p (b t) d", p=P)).then_inc(ld["x"], 16)
            sp.dma_start(ctx_sb[:, 4:8, :], ctx_t[:, 4:8, :]).then_inc(ld["ctx1"], 16)
            for r in range(4):
                rows = slice(32 * r, 32 * r + 32)
                sp.dma_start(w0[rows, :, 0, :], a["L0_xattn_Wq"].rearrange("(g p) d -> p g d", p=32)).then_inc(ld["w0"], 16)
            sp.dma_start(fw[:, :], a["L0_ffn_weight"]).then_inc(ld["fw"], 16)
            for r in range(4):
                rows = slice(32 * r, 32 * r + 32)
                for t, w in ((bk0, "L0_xattn_bk"), (bq0, "L0_xattn_bq")):
                    sp.dma_start(t[rows, :], a[w].rearrange("(g p) -> p g", p=32),
                                 allow_slow_non_contiguous=True).then_inc(ld["b0"], 16)
            sp.dma_start(bv0[:, :], a["L0_xattn_bv"].partition_broadcast(P)).then_inc(ld["bv0"], 16)
            sp.dma_start(m0_u8[:, :, :], a["mask_1x1xSxS2_bk0"].rearrange("a c (t p) k -> p (a c t) k", p=P)).then_inc(ld["m0"], 16)
            sp.dma_start(gates[:, 0:2], a["g_xattn"].partition_broadcast(P)).then_inc(ld["g"], 16)
            sp.dma_start(gates[:, 2:4], a["g_ffn"].partition_broadcast(P)).then_inc(ld["g"], 16)
            sp.dma_start(bo0[:, :], a["L0_xattn_bo"].partition_broadcast(P)).then_inc(ld["bv0"], 16)
            sp.dma_start(had[:, :], a["hadamard"]).then_inc(ld["had"], 16)
            for t, w in ((bk1, "L1_xattn_b_K"), (bq1, "L1_xattn_b_Q")):
                sp.dma_start(t[:, :], a[w].rearrange("(g p) -> p g", p=P),
                             allow_slow_non_contiguous=True).then_inc(ld["b1"], 16)
            sp.dma_start(bv1[:, :], a["L1_xattn_b_V"].partition_broadcast(P)).then_inc(ld["bv1"], 16)
            sp.dma_start(bo1[:, :], a["L1_xattn_b_out"].partition_broadcast(P)).then_inc(ld["bv1"], 16)
            for i, name in enumerate(("L1_xattn_W_Q", "L1_xattn_W_K", "L1_xattn_W_V")):
                sp.dma_start(w1[:, :, i, :], a[name].rearrange("(g p) d -> p g d", p=P)).then_inc(ld["w1"], 16)
            sp.dma_start(w1[:, :, 3, :], a["L1_xattn_W_out"].rearrange("o (g c) -> o g c", c=P)).then_inc(ld["w1"], 16)
            sp.dma_start(m1_u8[:, :, :, :].rearrange("p b t k -> p (b t) k"),
                         a["mask_BxSxS2_bk1"].rearrange("b (t p) k -> p (b t) k", p=P)).then_inc(ld["m1"], 16)
            sp.dma_start(wg[:, :], a["L1_ffn_Wg"]).then_inc(ld["moe"], 16)
            for s, w, shared in ((we1, "L1_ffn_W1", "L1_ffn_Ws1"), (we3, "L1_ffn_W3", "L1_ffn_Ws3")):
                sp.dma_start(s[:, 0:PAIRS, :].rearrange("p q (e h) -> p (q e) h", h=HID),
                             a[w].rearrange("e d h -> d e h")).then_inc(ld["moe"], 16)
                sp.dma_start(s[:, PAIRS, :], a[shared]).then_inc(ld["moe"], 16)
            sp.wait_ge(job_done, NUMBER["weights", 15] + 1)
            sp.dma_start(we2[:, 0:PAIRS, :], a["L1_ffn_W2"].rearrange("(q e) h d -> (e h) q d", e=2)).then_inc(ld["moe"], 16)
            sp.dma_start(we2[:, PAIRS, :], a["L1_ffn_Ws2"]).then_inc(ld["moe"], 16)
            for b in range(B):
                sp.wait_ge(y_used, 5 + b)
                sp.dma_start(out.rearrange("b (t p) d -> p b t d", p=P)[:, b, :, :],
                             x_sb[:, NQ * b:NQ * b + NQ, :]).then_inc(stored, 16)
            sp.wait_ge(stored, 16 * B)

        @block.gpsimd
        def _(pool):
            steps, told, late = [0], [0], [0]

            def step(ins):
                steps[0] += 1
                ins.then_inc(pool_step, 1)
                pool.wait_ge(pool_step, steps[0])

            def publish(ins):
                told[0] += 1
                ins.then_inc(const_ready, 1)
                pool.wait_ge(const_ready, told[0])

            def publish_late(ins):
                late[0] += 1
                ins.then_inc(late_ready, 1)
                pool.wait_ge(late_ready, late[0])

            pool.memset(w0[:, :, 2:4, :], 0.0).then_inc(zeros_ready, 1)
            step(pool.memset(ident[:, :], 0.0))
            publish(pool.affine_select(out=ident[:, :], in_=ident[:, :], compare_op=ALU.not_equal, fill=1.0,
                                       base=0, pattern=[[-1, P]], channel_multiplier=1))
            publish(pool.memset(neg_half[:, :], -0.5))
            for q, (sign_k, sign_q) in enumerate(((0.0, 0.0), (-1.0, 0.0), (0.0, -1.0), (-1.0, -1.0))):
                rows = slice(32 * q, 32 * q + 32)
                publish(pool.memset(lo_k[rows, :], sign_k))
                publish(pool.memset(lo_q[rows, :], sign_q))
            step(pool.memset(head_row[:, :], 1.0))
            for r in range(4):
                rows = head_row[32 * r:32 * r + 32, :]
                step(pool.affine_select(out=rows, in_=rows, compare_op=ALU.is_ge, fill=0.0, base=0,
                                        pattern=[[-8, 4]], channel_multiplier=1))
                step(pool.affine_select(out=rows, in_=rows, compare_op=ALU.is_ge, fill=0.0, base=7,
                                        pattern=[[8, 4]], channel_multiplier=-1))
            pool.wait_ge(zeros_ready, 1)
            pool.wait_ge(ld["wo0"], 16)
            pool.tensor_copy(w0[:, :, 3, :].rearrange("p g (j c) -> p g j c", c=32)[:, :, :, 0:8],
                             wo0[:, :].rearrange("p (g j c) -> p g j c", j=4, c=8)).then_inc(wo0_ready, 1)
            publish_late(pool.memset(val[:, :, :, :], 0.0))
            publish_late(pool.memset(q1_high[64:P, :, 0, :].bitcast(F32), 0.0))
            publish_late(pool.memset(q1_high[0:64, :, 1, :].bitcast(F32), 0.0))

            def rstd_of(n, b):
                pool.wait_ge(var_ready, LN[n, b] + 1)
                ts = ln_tiles(n, b)
                cols = slice(ts[0], ts[-1] + 1)
                pool.tensor_tensor(rstd[:, cols], veps[:, cols], neg_half[:, cols], ALU.pow).then_inc(rstd_ready, 1)

            def norm(u):
                pool.wait_ge(recipped, u + 1)
                p = probs[:, u % NP, :]
                pool.tensor_scalar(p, p, rsum[:, u % NCOL:u % NCOL + 1], 1.0, ALU.mult, ALU.mult).then_inc(normed, 1)

            def q_stack(m):
                pool.wait_ge(*freed(("q", m)))
                if m >= 2:
                    pool.wait_ge(scored, BLOCKS[m - 2].end)
                for j in range(4):
                    pool.tensor_scalar(q0[:, m % 2, j, :], stack_f[:, :], head_row[:, j:j + 1], 1.0,
                                       ALU.mult, ALU.mult).then_inc(q0_ready, 1)

            rstd_of(0, 0)
            pool.wait_ge(ld["m0"], 16)
            pool.tensor_scalar(mask0[:, :, :], m0_u8[:, :, :], FAR, -FAR, ALU.mult, ALU.add).then_inc(mask_ready[0], 1)
            q_stack(0)
            for t in range(-LEAD, TOTAL):
                if 0 <= t + LEAD - 3 < TOTAL:
                    norm(t + LEAD - 3)
                for job in PLAN.get(t - 1, ()):
                    if job[0] == "q" and BLOCKS[job[1]].layer == 0:
                        q_stack(job[1])
                for b in range(B):
                    if t == Y_DONE[0, b] + 2:
                        rstd_of(1, b)
                    if t == Y_DONE[0, b] + 15:
                        rstd_of(2, b)
                if t == Y_DONE[1, 0] + 2:
                    rstd_of(3, 0)
                if t >= 12 and t % 2 == 0 and t < 12 + 2 * B * NQ:
                    pool.wait_ge(ld["m1"], 16)
                    b, i = divmod((t - 12) // 2, NQ)
                    pool.tensor_scalar(mask1[:, b, i, :], m1_u8[:, b, i, :], -FAR, 0.0, ALU.mult,
                                       ALU.add).then_inc(mask_ready[1], 1)
                if t == TOTAL // 2 + 8:
                    pool.wait_ge(normed, t + LEAD - 2)
                    publish_late(pool.memset(ones32[:, :], 1.0))
                    publish_late(pool.memset(ones_b[:, :], 1.0))
                    publish_late(pool.affine_select(out=before_b[:, :], in_=ones_b[:, :], compare_op=ALU.is_gt,
                                                    fill=0.0, base=0, pattern=[[1, P]], channel_multiplier=-1))
                    publish_late(pool.memset(gateT[64:P, :].bitcast(F32), 0.0))
            rstd_of(3, 1)

        @block.scalar
        def _(act):
            act.dma_start(wo0[:, :], a["L0_xattn_Wo"]).then_inc(ld["wo0"], 16)
            act.wait_ge(zeros_ready, 1)
            for j in range(4):
                act.dma_start(w0[32 * j:32 * j + 8, :, 2, :],
                              a["L0_xattn_Wv"].rearrange("(g j p) d -> j p g d", j=4, p=8)[j]).then_inc(ld["w0"], 16)

            def exp(u):
                act.wait_ge(maxed, u + 1)
                if u >= NP:
                    act.wait_ge(turned, u - NP + 1)
                if u >= NCOL:
                    act.wait_ge(recipped, u - NCOL + 1)
                c = u % NCOL
                act.activation(probs[:, u % NP, :], masked[:, u % NS, :], ACT.Exp, scale=-1.0,
                               bias=neg_max[:, c:c + 1], accum_out=sums[:, c:c + 1]).then_inc(exped, 1)

            def copy_turned(u):
                k, h, qt = unit(u)
                act.wait_ge(turned, u + 1)
                if k.m >= 2:
                    act.wait_ge(mixed, k.m - 1)
                act.activation(probsT[:, k.m % 2, h, :, qt * P:qt * P + P],
                               turn_bank[u % 2][:, :].rearrange("p (k q) -> p k q", q=P),
                               ACT.Copy).then_inc(copied[u % 2], 1)

            def mix_copy(k):
                act.wait_ge(mixed, k.m + 1)
                if k.m >= 2:
                    act.wait_ge(projected_out, k.m - 1)
                act.activation(mixT[:, k.m % 2, :], mix_bank[:, 0:SQ], ACT.Copy).then_inc(mix_copied, 1)

            def job(j):
                name, n = j[0], NUMBER[j]
                if name in ("v", "ffn", "rank"):
                    return
                job_bank, free = job_banks[PLACE[j][0]], job_free[PLACE[j][0]]
                act.wait_ge(job_done, n + 1)
                if name == "weights":
                    k = BLOCKS[j[1]]
                    act.activation((w0T, w1T)[k.layer][:, k.g, :, :].rearrange("p a c -> p (a c)"), job_bank[:, :],
                                   ACT.Copy).then_inc(free, 1)
                elif name in ("k", "q"):
                    k = BLOCKS[j[1]]
                    cols = SK if name == "k" else SQ
                    i, row = k.m % 2, slice(k.g, k.g + 1)
                    if k.layer == 0:
                        high, sign, bias = ((high_q, lo_q, minus_bq0), (high_k, lo_k, minus_bk0))[name == "k"]
                        if k.m == 0:
                            act.wait_ge(minus_ready, 2)
                        else:
                            act.wait_ge(*freed((name, k.m - 1)))
                        act.activation(high[:, :], job_bank[:, 0:cols], ACT.Identity, bias=bias[:, row],
                                       scale=sign[:, 0:1]).then_inc(high_ready, 1)
                        return
                    bias = (bq1, bk1)[name == "k"]
                    act.wait_ge(ld["b1"], 32)
                    act.wait_ge(scored, BLOCKS[k.m - 2].end)
                    act.wait_ge(late_ready, 3)
                    own = [slice(64 * h, 64 * h + 64) for h in range(2)]
                    if name == "k":
                        act.activation(k1_high[:, i, :], job_bank[:, :], ACT.Identity, bias=bias[:, row]).then_inc(high_ready, 1)
                        act.wait_ge(high_ready, HIGHS[j])
                        for h in range(2):
                            act.activation(k1_both[own[1 - h], i, h, :], k1_high[own[h], i, :], ACT.Copy).then_inc(cross_ready, 1)
                    else:
                        for h in range(2):
                            act.activation(q1_high[own[h], i, h, :], job_bank[own[h], 0:cols], ACT.Identity,
                                           bias=bias[own[h], row]).then_inc(high_ready, 1)
                elif name == "ln":
                    ts = ln_tiles(*j[1:])
                    act.activation(xnT[:, j[1] % 3, ts[0] * P:(ts[-1] + 1) * P], job_bank[:, 0:len(ts) * P],
                                   ACT.Copy).then_inc(free, 1)
                elif name == "rotate":
                    act.activation(xh[:, :, :].rearrange("p t c -> p (t c)"), job_bank[:, 0:SQ], ACT.Copy).then_inc(free, 1)
                elif name == "turn_fw":
                    act.activation(fwT[:, :], job_bank[:, 0:P], ACT.Copy).then_inc(free, 1)
                elif name == "turn_xq":
                    act.activation(xqT[:, :], job_bank[:, 0:SQ], ACT.Copy).then_inc(free, 1)
                elif name == "logits":
                    act.wait_ge(lmax_ready, j[1] + 1)
                    for t in range(NQ):
                        ins = act.activation(ex[:, t, :], job_bank[:, t * EXPERTS:(t + 1) * EXPERTS], ACT.Exp,
                                             bias=lg[:, t:t + 1], accum_out=ls[:, t:t + 1])
                        ins.then_inc(*((free, 1) if t == NQ - 1 else (half_done, 1)))
                elif name == "turn_gate":
                    act.activation(gate_full[:, :], job_bank[0:2 * EXPERTS, 0:SQ], ACT.Copy).then_inc(gate_copied, 1)
                    act.activation(gate_hi[:, :], job_bank[0:2 * EXPERTS, 0:SQ], ACT.Copy).then_inc(free, 1)

            for i in range(2):
                act.wait_ge(ctx_turned, i + 1)
                act.activation(ctxT[:, 512 * i:512 * i + 512], turn_bank[i][:, :], ACT.Copy).then_inc(ctxT_ready, 1)
            for j in BEFORE:
                job(j)
            act.wait_ge(ld["g"], 32)
            act.activation(tanh_g[:, :], gates[:, :], ACT.Tanh).then_inc(tanh_ready, 1)
            def attend(t):
                for k in BLOCKS:
                    if t == k.copy_at:
                        mix_copy(k)
                for j in PLAN.get(t - 1, ()):
                    job(j)
                if 0 <= t + LEAD - 2 < TOTAL:
                    exp(t + LEAD - 2)
                if 0 <= t - 1 < TOTAL and on_act(t - 1):
                    copy_turned(t - 1)

            for t in range(-LEAD, EXPERTS_AT):
                attend(t)
                if t in SPREAD_AT:
                    e = SPREAD_AT.index(t) * SPREAD_STEP
                    for half in range(2):
                        rows, c = slice(EXPERTS * half, EXPERTS * (half + 1)), EXPERTS * half + e
                        act.activation(spread[rows, e:e + SPREAD_STEP, :],
                                       ident[rows, c:c + SPREAD_STEP].unsqueeze(2).to_broadcast([EXPERTS, SPREAD_STEP, HID]),
                                       ACT.Copy).then_inc(spread_ready, 1)
            for b in range(B):
                for p in range(HALVES):
                    n = b * HALVES + p
                    if b == 0:
                        attend(EXPERTS_AT + p)
                    act.wait_ge(u_ready, n + 1)
                    if n >= 2:
                        act.wait_ge(hid_ready, n - 1)
                    act.activation(silu[:, n % 2, :], u_bank[n % 2][:, 0:SQ], ACT.Silu).then_inc(silu_ready, 1)
                    if b == 0:
                        for j in AFTER.get(EXPERTS_AT + p - 1, ()):
                            job(j)

        @block.vector
        def _(dve):
            steps = [0]

            def step(ins):
                steps[0] += 1
                ins.then_inc(dve_step, 1)
                dve.wait_ge(dve_step, steps[0])

            def steps_of(instructions):
                for ins in instructions:
                    steps[0] += 1
                    ins.then_inc(dve_step, 1)
                dve.wait_ge(dve_step, steps[0])

            def ln_stats(n, b):
                ts = ln_tiles(n, b)
                steps_of([dve.bn_stats(stats[:, t, :], x_sb[:, t, :]) for t in ts])
                steps_of([dve.bn_aggr(mv[:, t, :], stats[:, t, :]) for t in ts])
                cols = slice(ts[0], ts[-1] + 1)
                dve.tensor_scalar(veps[:, cols], mv[:, cols, 1], LN_EPS, None, ALU.add).then_inc(var_ready, 1)

            def ln_norm(n, b):
                dve.wait_ge(rstd_ready, LN[n, b] + 1)
                for t in ln_tiles(n, b):
                    dve.tensor_scalar(xn[:, t, :], x_sb[:, t, :], mv[:, t, 0:1], rstd[:, t:t + 1],
                                      ALU.subtract, ALU.mult).then_inc(xn_ready, 1)

            def add_y(layer, b, bias, gate):
                x = x_sb[:, NQ * b:NQ * b + NQ, :]
                y = (moe_bank[b][:, 0:SQ] if layer == 2 else y_bank[:, b * SQ:b * SQ + SQ]).rearrange("p (t c) -> p t c", c=P)
                if bias is not None:
                    step(dve.tensor_tensor(tmp[:, :, :], y, bias[:, :].unsqueeze(1).to_broadcast([P, NQ, P]), ALU.add))
                    y = tmp[:, :, :]
                dve.scalar_tensor_tensor(out=x, in0=y, scalar=tanh_g[:, gate:gate + 1], in1=x,
                                         op0=ALU.mult, op1=ALU.add).then_inc(y_used, 1)
                dve.wait_ge(y_used, 2 * layer + b + 1)

            def mask_max(u):
                k, h, qt = unit(u)
                dve.wait_ge(scored, u + 1)
                if u >= NS:
                    dve.wait_ge(exped, u - NS + 1)
                mask = mask0[:, qt, :] if k.layer == 0 else mask1[:, k.b, qt, :]
                c = u % NCOL
                dve.tensor_tensor_reduce(out=masked[:, u % NS, :], in0=score_bank[u % 2][:, :], in1=mask,
                                         scale=-float(k.depth) ** -0.5, scalar=3.0e38, op0=ALU.add, op1=ALU.min,
                                         accum_out=neg_max[:, c:c + 1]).then_inc(maxed, 1)

            def recip(u):
                c = u % NCOL
                dve.wait_ge(exped, u + 1)
                if u >= NCOL:
                    dve.wait_ge(normed, u - NCOL + 1)
                dve.reciprocal(rsum[:, c:c + 1], sums[:, c:c + 1]).then_inc(recipped, 1)

            def copy_turned(u):
                k, h, qt = unit(u)
                dve.wait_ge(turned, u + 1)
                if k.m >= 2:
                    dve.wait_ge(mixed, k.m - 1)
                dve.tensor_copy(probsT[:, k.m % 2, h, :, qt * P:qt * P + P],
                                turn_bank[u % 2][:, :].rearrange("p (k q) -> p k q", q=P)).then_inc(copied[u % 2], 1)

            def job(j):
                name, n = j[0], NUMBER[j]
                job_bank, free = job_banks[PLACE[j][0]], job_free[PLACE[j][0]]
                if name == "v":
                    k = BLOCKS[j[1]]
                    dve.wait_ge(job_done, n + 1)
                    if k.m >= NV:
                        dve.wait_ge(mixed, k.m - NV + 1)
                    if k.layer == 0:
                        dst = val[:, k.m % NV, :, :].rearrange("p k (j c) -> p k j c", c=32)[:, :, :, 0:8]
                        src = job_bank[:, :].rearrange("p (k j c) -> p k j c", j=4, c=32)[:, :, :, 0:8]
                        bias = bv0[:, 32 * k.g:32 * k.g + 32].rearrange("p (j c) -> p j c", c=8).unsqueeze(1)\
                            .to_broadcast([P, NK, 4, 8])
                    else:
                        dve.wait_ge(ld["bv1"], 32)
                        dst = val[:, k.m % NV, :, :]
                        src = job_bank[:, :].rearrange("p (k c) -> p k c", c=P)
                        bias = bv1[:, P * k.g:P * k.g + P].unsqueeze(1).to_broadcast([P, NK, P])
                    dve.tensor_tensor(dst, src, bias, ALU.add).then_inc(free, 1)
                elif name in ("k", "q"):
                    k = BLOCKS[j[1]]
                    i, row = k.m % 2, slice(k.g, k.g + 1)
                    if k.layer == 0:
                        if name == "k":
                            if k.m >= 2:
                                dve.wait_ge(scored, BLOCKS[k.m - 2].end)
                            dst, high, bias = k0[:, i, :], high_k, bk0
                        else:
                            if k.m >= 1:
                                dve.wait_ge(q0_ready, 4 * k.m)
                            dst, high, bias = stack_f[:, :], high_q, bq0
                        cols = SK if name == "k" else SQ
                        dve.wait_ge(high_ready, HIGHS[j])
                        dve.scalar_tensor_tensor(out=dst, in0=job_bank[:, 0:cols], scalar=bias[:, row],
                                                 in1=high[:, :].bitcast(F32), op0=ALU.add, op1=ALU.add).then_inc(free, 1)
                        return
                    own = [slice(64 * h, 64 * h + 64) for h in range(2)]
                    if name == "k":
                        dve.wait_ge(scored, BLOCKS[k.m - 2].end)
                        dve.wait_ge(high_ready, HIGHS[j])
                        for h in range(2):
                            ins = dve.scalar_tensor_tensor(out=k1_both[own[h], i, h, :], in0=job_bank[own[h], :],
                                                           scalar=bk1[own[h], row], in1=k1_high[own[h], i, :].bitcast(F32),
                                                           op0=ALU.add, op1=ALU.subtract)
                            ins.then_inc(*((free, 1) if h == 1 else (half_dve, 1)))
                    else:
                        for h in range(2):
                            dve.wait_ge(high_ready, HIGHS[j] - 1 + h)
                            ins = dve.scalar_tensor_tensor(out=q1_both[own[1 - h], i, h, :], in0=job_bank[own[h], 0:SQ],
                                                           scalar=bq1[own[h], row], in1=q1_high[own[h], i, h, :].bitcast(F32),
                                                           op0=ALU.add, op1=ALU.subtract)
                            ins.then_inc(*((free, 1) if h == 1 else (half_dve, 1)))
                        for h in range(2):
                            dve.tensor_copy(q1_both[own[h], i, h, :], q1_high[own[h], i, h, :]).then_inc(own_ready, 1)

            def quantise(b, part):
                inv = qs[:, 2, :].unsqueeze(2).to_broadcast([P, NQ, P])
                scl = qs[:, 1, :].unsqueeze(2).to_broadcast([P, NQ, P])
                rounder = 1.5 * 2.0 ** 23
                if part == 0:
                    dve.wait_ge(*freed(("rotate", b)))
                    step(dve.tensor_reduce(qs[:, 0, :], xh[:, :, :], X, ALU.max, apply_absolute_value=True))
                    step(dve.tensor_scalar(qs[:, 1, :], qs[:, 0, :], 1e-5, 1.0 / 7.0, ALU.max, ALU.mult))
                    step(dve.reciprocal(qs[:, 2, :], qs[:, 1, :]))
                    step(dve.tensor_tensor(tmp[:, :, :], xh[:, :, :], inv, ALU.mult))
                    step(dve.tensor_scalar(tmp[:, :, :], tmp[:, :, :], rounder, -rounder, ALU.add, ALU.add))
                else:
                    step(dve.tensor_scalar(tmp[:, :, :], tmp[:, :, :], -8.0, 7.0, ALU.max, ALU.min))
                    step(dve.tensor_tensor(tmp[:, :, :], tmp[:, :, :], scl, ALU.mult))
                    step(dve.tensor_tensor(tmp[:, :, :], tmp[:, :, :], xh[:, :, :], ALU.subtract))
                    dve.tensor_tensor(xq[:, :, :], xh[:, :, :], tmp[:, :, :], ALU.add).then_inc(xq_ready, 1)

            def ternary(part):
                if part == 0:
                    dve.wait_ge(ld["fw"], 16)
                    step(dve.tensor_reduce(fcol[:, 0:1], fw[:, :], X, ALU.add, apply_absolute_value=True))
                    step(dve.tensor_scalar(fcol[:, 1:2], fcol[:, 0:1], 1.0 / P, 1e-5, ALU.mult, ALU.max))
                    step(dve.reciprocal(fcol[:, 2:3], fcol[:, 1:2]))
                elif part == 1:
                    step(dve.tensor_scalar(fq[:, :], fw[:, :], fcol[:, 2:3], None, ALU.mult))
                    steps_of([dve.tensor_scalar(fs[:, 0, :], fq[:, :], 0.5, None, ALU.is_gt),
                              dve.tensor_scalar(fs[:, 1, :], fq[:, :], -0.5, None, ALU.is_lt)])
                elif part == 2:
                    step(dve.tensor_tensor(fs[:, 0, :], fs[:, 0, :], fs[:, 1, :], ALU.subtract))
                    step(dve.scalar_tensor_tensor(out=fs[:, 1, :], in0=fs[:, 0, :], scalar=fcol[:, 1:2], in1=fw[:, :],
                                                  op0=ALU.mult, op1=ALU.subtract))
                    dve.tensor_tensor(fq[:, :], fw[:, :], fs[:, 1, :], ALU.add).then_inc(fw_ready, 1)

            def feed_forward(b, o):
                if o == 0:
                    dve.wait_ge(projected_out, 4 * b + 4)
                    dve.wait_ge(tanh_ready, 1)
                    add_y(0, b, bo0, 0)
                if o == 1:
                    ln_stats(1, b)
                if o == 3:
                    ln_norm(1, b)
                if o in (9, 10):
                    quantise(b, o - 9)
                if o == 14:
                    j = ("ffn", b)
                    n = NUMBER[j]
                    job_bank, free = job_banks[PLACE[j][0]], job_free[PLACE[j][0]]
                    dve.wait_ge(job_done, n + 1)
                    x = x_sb[:, NQ * b:NQ * b + NQ, :]
                    dve.scalar_tensor_tensor(out=x, in0=job_bank[:, 0:SQ].rearrange("p (t c) -> p t c", c=P),
                                             scalar=tanh_g[:, 2:3], in1=x, op0=ALU.mult, op1=ALU.add).then_inc(free, 1)
                    dve.wait_ge(*freed(("ffn", b)))
                if o == 15:
                    ln_stats(2, b)
                if o == 16:
                    ln_norm(2, b)

            def router(b, o):
                if o == 0:
                    dve.wait_ge(projected_out, 8 + 8 * b + 8)
                    add_y(1, b, bo1, 1)
                if o == 1:
                    ln_stats(3, b)
                if o == 3:
                    ln_norm(3, b)
                if o == 7 - b:
                    dve.wait_ge(job_done, NUMBER["logits", b] + 1)
                    job_bank = job_banks[PLACE["logits", b][0]]
                    logits = job_bank[:, 0:NQ * EXPERTS].rearrange("p (t e) -> p t e", e=EXPERTS)
                    dve.tensor_reduce(lg[:, :], logits, X, ALU.max, negate=True).then_inc(lmax_ready, 1)
                if o == 8:
                    dve.wait_ge(late_ready, 7)
                    dve.wait_ge(*freed(("logits", b)))
                    step(dve.reciprocal(lr[:, :], ls[:, :]))
                    step(dve.tensor_tensor(sc[:, :, :], ex[:, :, :], lr[:, :].unsqueeze(2).to_broadcast([P, NQ, EXPERTS]), ALU.mult))
                    steps_of([dve.max(top8[:, t, :], sc[:, t, :]) for t in range(NQ)])
                fourth = top8[:, :, TOP - 1:TOP].to_broadcast([P, NQ, EXPERTS])
                if o == 9:
                    steps_of([dve.tensor_tensor(above[:, :, :], sc[:, :, :], fourth, ALU.is_gt),
                              dve.tensor_tensor(equal[:, :, :], sc[:, :, :], fourth, ALU.is_equal)])
                    step(dve.tensor_reduce(lg[:, :], above[:, :, :], X, ALU.add))
                    step(dve.tensor_scalar(room[:, :], lg[:, :], -1.0, float(TOP), ALU.mult, ALU.add))
                if o == 10:
                    steps_of([dve.tensor_tensor_scan(run[:, t, :], ones32[:, :], equal[:, t, :], 0.0, ALU.mult, ALU.add)
                              for t in range(NQ)])
                    step(dve.tensor_tensor(run[:, :, :], run[:, :, :], room[:, :].unsqueeze(2).to_broadcast([P, NQ, EXPERTS]), ALU.is_le))
                    step(dve.tensor_tensor(run[:, :, :], run[:, :, :], equal[:, :, :], ALU.mult))
                    step(dve.tensor_tensor(sel[:, :, :], run[:, :, :], above[:, :, :], ALU.add))
                    dve.tensor_copy(sel_b[:, NQ * b:NQ * b + NQ, :], sel[:, :, :]).then_inc(sel_ready, 1)
                if o == 12:
                    j = ("rank", b)
                    n = NUMBER[j]
                    job_bank, free = job_banks[PLACE[j][0]], job_free[PLACE[j][0]]
                    dve.wait_ge(job_done, n + 1)
                    rank = job_bank[:, 0:NQ * EXPERTS].rearrange("p (t e) -> p t e", e=EXPERTS)
                    dve.scalar_tensor_tensor(out=kept[:, :, :], in0=rank, scalar=float(CAP), in1=sel[:, :, :],
                                             op0=ALU.is_lt, op1=ALU.mult).then_inc(free, 1)
                    dve.wait_ge(*freed(("rank", b)))
                    for i in range(2):
                        dve.tensor_tensor(wgt[:, :, i, :], kept[:, :, :], sc[:, :, :], ALU.mult).then_inc(wgt_ready, 1)
                if o == 14:
                    dve.wait_ge(*freed(("turn_gate", b)))
                    dve.scalar_tensor_tensor(out=gateT[0:2 * EXPERTS, b * SQ:b * SQ + SQ], in0=gate_hi[:, :].bitcast(F32),
                                             scalar=lo_k[0:2 * EXPERTS, 0:1], in1=gate_full[:, :],
                                             op0=ALU.mult, op1=ALU.add).then_inc(gateT_ready, 1)

            dve.wait_ge(ld["x"], 16)
            ln_stats(0, 0)
            ln_norm(0, 0)
            dve.wait_ge(const_ready, 10)
            dve.wait_ge(ld["b0"], 16 * 8)
            for dst, bias, sign in ((minus_bk0, bk0, lo_k), (minus_bq0, bq0, lo_q)):
                dve.tensor_scalar(dst[:, :], bias[:, :], sign[:, 0:1], None, ALU.mult).then_inc(minus_ready, 1)
            ternary(0)
            ternary(1)
            dve.wait_ge(late_ready, 1)
            for n, j in enumerate(BEFORE):
                if j[0] == "v":
                    dve.wait_ge(ld["bv0"], 32)
                job(j)
                if n == 1:
                    ternary(2)
            dve.wait_ge(mask_ready[0], 1)
            for t in range(-LEAD, EXPERTS_AT):
                if t + LEAD - 1 == TOTAL // 2:
                    dve.wait_ge(mask_ready[1], B * NQ)
                if 0 <= t + LEAD - 1 < TOTAL:
                    mask_max(t + LEAD - 1)
                if 0 <= t + LEAD - 3 < TOTAL:
                    recip(t + LEAD - 3)
                for j in PLAN.get(t - 1, ()):
                    job(j)
                if 0 <= t - 1 < TOTAL and not on_act(t - 1):
                    copy_turned(t - 1)
                for b in range(B):
                    feed_forward(b, t - Y_DONE[0, b])
                router(0, t - Y_DONE[1, 0])
            for b in range(B):
                for p in range(HALVES):
                    n = b * HALVES + p
                    i = n % 2
                    dve.wait_ge(silu_ready, n + 1)
                    dve.wait_ge(v_ready, n + 1)
                    if n >= 2:
                        dve.wait_ge(down_done, n - 1)
                    if p < PAIRS:
                        dve.tensor_tensor(prod[:, i, :], v_bank[i][:, 0:SQ], silu[:, i, :], ALU.mult).then_inc(prod_ready, 1)
                        dve.wait_ge(g_ready, b * PAIRS + p + 1)
                        dve.wait_ge(prod_ready, b * PAIRS + p + 1)
                        dve.tensor_tensor(hidT[:, i, :], g_bank[:, 0:SQ], prod[:, i, :], ALU.mult).then_inc(hid_ready, 1)
                    else:
                        dve.tensor_tensor(hidT[:, i, :], v_bank[i][:, 0:SQ], silu[:, i, :], ALU.mult).then_inc(hid_ready, 1)
                    if b == 0:
                        router(1, EXPERTS_AT + p - Y_DONE[1, 1])
                dve.wait_ge(down_done, (b + 1) * HALVES)
                add_y(2, b, None, 3)

        @block.tensor
        def _(pe):
            def turn_tiles(dst, tiles, rows=P):
                for t, src in enumerate(tiles):
                    ins = pe.transpose(dst[0:rows, t * P:t * P + P], src, ident[:, :])
                return ins

            def job(j):
                name, (i, before) = j[0], PLACE[j]
                job_bank = job_banks[i]
                if before:
                    pe.wait_ge(job_free[i], before)
                if name in ("weights", "k", "q", "v"):
                    k = BLOCKS[j[1]]
                    wT = (w0T, w1T)[k.layer][:, k.g, :, :]
                    if name != "weights":
                        pe.wait_ge(*freed(("weights", k.m - k.b * k.groups)))
                    if name == "weights":
                        if k.layer == 1 and k.g == 0:
                            pe.wait_ge(ld["w1"], 64)
                        w = (w0, w1)[k.layer]
                        ins = turn_tiles(job_bank, [w[:, k.g, i, :] for i in range(4)])
                    elif name == "q":
                        pe.wait_ge(*freed(("ln", 2 * k.layer, k.b * k.layer)))
                        ins = pe.matmul(job_bank[:, 0:SQ], wT[:, 0, :], xnT[:, 2 * k.layer, k.b * SQ:k.b * SQ + SQ],
                                        start=True, stop=True)
                    elif name == "k":
                        ins = pe.matmul(job_bank[:, :], wT[:, 1, :], ctxT[:, k.b * SK:k.b * SK + SK], start=True, stop=True)
                    else:
                        for i in range(NK):
                            c = (k.b * NK + i) * P
                            ins = pe.matmul(job_bank[:, i * P:i * P + P], ctxT[:, c:c + P], wT[:, 2, :], start=True, stop=True)
                elif name == "ln":
                    pe.wait_ge(xn_ready, xn_count(*j[1:]))
                    ins = turn_tiles(job_bank, [xn[:, t, :] for t in ln_tiles(*j[1:])])
                elif name == "rotate":
                    pe.wait_ge(ld["had"], 16)
                    pe.wait_ge(*freed(("ln", 1, j[1])))
                    b = j[1]
                    for t in range(NQ):
                        c = b * SQ + t * P
                        ins = pe.matmul(job_bank[:, t * P:t * P + P], xnT[:, 1, c:c + P], had[:, :], start=True, stop=True)
                elif name == "turn_xq":
                    pe.wait_ge(xq_ready, j[1] + 1)
                    ins = turn_tiles(job_bank, [xq[:, t, :] for t in range(NQ)])
                elif name == "turn_fw":
                    pe.wait_ge(fw_ready, 1)
                    ins = turn_tiles(job_bank, [fq[:, :]])
                elif name == "ffn":
                    pe.wait_ge(*freed(("turn_fw",)))
                    pe.wait_ge(*freed(("turn_xq", j[1])))
                    for t in range(NQ):
                        ins = pe.matmul(job_bank[:, t * P:t * P + P], xqT[:, t * P:t * P + P], fwT[:, :], start=True, stop=True)
                elif name == "logits":
                    pe.wait_ge(ld["moe"], 16 * 7)
                    pe.wait_ge(*freed(("ln", 3, j[1])))
                    for t in range(NQ):
                        c = j[1] * SQ + t * P
                        ins = pe.matmul(job_bank[:, t * EXPERTS:(t + 1) * EXPERTS], xnT[:, 0, c:c + P], wg[:, :],
                                        start=True, stop=True)
                elif name == "rank":
                    pe.wait_ge(sel_ready, j[1] + 1)
                    for i in range(NQ):
                        t = j[1] * NQ + i
                        for s in range(t + 1):
                            ins = pe.matmul(job_bank[:, i * EXPERTS:(i + 1) * EXPERTS],
                                            (before_b if s == t else ones_b)[:, :], sel_b[:, s, :],
                                            start=(s == 0), stop=(s == t))
                else:
                    pe.wait_ge(wgt_ready, 2 * j[1] + 2)
                    ins = turn_tiles(job_bank, [wgt[:, t, :, :].rearrange("p a e -> p (a e)") for t in range(NQ)],
                                     rows=2 * EXPERTS)
                ins.then_inc(job_done, 1)

            def scores(u):
                k, h, qt = unit(u)
                dst = score_bank[u % 2][:, :]
                i, q = k.m % 2, slice(qt * P, qt * P + P)
                pe.wait_ge(*freed(("k", k.m)))
                if u >= 2:
                    pe.wait_ge(maxed, u - 1)
                if k.layer == 0:
                    pe.wait_ge(q0_ready, 4 * k.m + h + 1)
                    pe.matmul(dst, q0[:, i, h, q], k0[:, i, :], start=True, stop=True).then_inc(scored, 1)
                else:
                    pe.wait_ge(*freed(("q", k.m)))
                    pe.wait_ge(own_ready, 2 * (k.m - 7))
                    pe.wait_ge(cross_ready, 2 * (k.m - 7))
                    pe.matmul(dst, q1_high[:, i, h, q], k1_high[:, i, :], start=True, stop=False)
                    pe.matmul(dst, q1_both[:, i, h, q], k1_both[:, i, h, :], start=False, stop=True).then_inc(scored, 1)

            def turn(u):
                pe.wait_ge(normed, u + 1)
                if u >= 2:
                    pe.wait_ge(copied[u % 2], u // 2)
                turn_tiles(turn_bank[u % 2], [probs[:, u % NP, i * P:i * P + P] for i in range(NK)]).then_inc(turned, 1)

            def mix(k, half):
                if half == 0:
                    for i in range(2):
                        pe.wait_ge(copied[i], k.end // 2)
                    pe.wait_ge(*freed(("v", k.m)))
                    if k.m >= 1:
                        pe.wait_ge(mix_copied, k.m)
                w = k.width
                for i in range(half * NK // 2, (half + 1) * NK // 2):
                    for h in range(k.heads):
                        ins = pe.matmul(mix_bank[w * h:w * h + w, 0:SQ], val[:, k.m % NV, i, w * h:w * h + w],
                                        probsT[:, k.m % 2, h, i, :], start=(i == 0), stop=(i == NK - 1))
                if half == 1:
                    ins.then_inc(mixed, 1)

            def project_out(k):
                pe.wait_ge(mix_copied, k.m + 1)
                if k.g == 0 and (k.layer or k.b):
                    pe.wait_ge(y_used, 2 * k.layer + k.b)
                for t in range(NQ):
                    c = k.b * SQ + t * P
                    ins = pe.matmul(y_bank[:, c:c + P], mixT[:, k.m % 2, t * P:t * P + P],
                                    (w0T, w1T)[k.layer][:, k.g, 3, :], start=(k.g == 0 and t == 0),
                                    stop=(k.g == k.groups - 1), skip_group_check=True)
                ins.then_inc(projected_out, 1)

            pe.wait_ge(const_ready, 1)
            for i in range(2):
                pe.wait_ge(ld[f"ctx{i}"], 16)
                turn_tiles(turn_bank[i], [ctx_sb[:, 4 * i + t, :] for t in range(4)]).then_inc(ctx_turned, 1)
            pe.wait_ge(ld["w0"], 16 * 12)
            pe.wait_ge(wo0_ready, 1)
            for n, j in enumerate(BEFORE):
                job(j)
                if n == 0:
                    pe.wait_ge(ctxT_ready, 2)
            def attend(t):
                if 0 <= t + LEAD < TOTAL:
                    scores(t + LEAD)
                for j in PLAN.get(t, ()):
                    job(j)
                for k in BLOCKS:
                    for half in range(2):
                        if t == k.mix_at[half]:
                            mix(k, half)
                    if t == k.out_at:
                        project_out(k)
                if 0 <= t < TOTAL:
                    turn(t)

            for t in range(-LEAD, EXPERTS_AT):
                attend(t)

            def down(n):
                b, p = divmod(n, HALVES)
                pe.wait_ge(hid_ready, n + 1)
                for t in range(NQ):
                    ins = pe.matmul(moe_bank[b][:, t * P:t * P + P], hidT[:, n % 2, t * P:t * P + P], we2[:, p, :],
                                    start=(p == 0 and t == 0), stop=(p == PAIRS), skip_group_check=True)
                ins.then_inc(down_done, 1)

            pe.wait_ge(maxed, TOTAL)
            for i in range(2):
                pe.wait_ge(copied[i], TOTAL // 2)
            pe.wait_ge(spread_ready, 2 * len(SPREAD_AT))
            for b in range(B):
                xT = xnT[:, 0, b * SQ:b * SQ + SQ]
                for p in range(HALVES):
                    n = b * HALVES + p
                    i = n % 2
                    if b == 0:
                        attend(EXPERTS_AT + p)
                    if n == 0:
                        pe.wait_ge(gateT_ready, 1)
                    if n >= 2:
                        pe.wait_ge(silu_ready, n - 1)
                    pe.matmul(u_bank[i][:, 0:SQ], we1[:, p, :], xT, start=True, stop=True).then_inc(u_ready, 1)
                    if n >= 2:
                        pe.wait_ge(hid_ready, n - 1)
                    pe.matmul(v_bank[i][:, 0:SQ], we3[:, p, :], xT, start=True, stop=True).then_inc(v_ready, 1)
                    if p < PAIRS:
                        if p == 0:
                            pe.wait_ge(gateT_ready, b + 1)
                        if n >= 1:
                            pe.wait_ge(hid_ready, n)
                        pe.matmul(g_bank[:, 0:SQ], spread[:, 2 * p:2 * p + 2, :].rearrange("p e h -> p (e h)"),
                                  gateT[:, b * SQ:b * SQ + SQ], start=True, stop=True).then_inc(g_ready, 1)
                    if n >= 1:
                        down(n - 1)
                    if b == 0:
                        for j in AFTER.get(EXPERTS_AT + p, ()):
                            job(j)
            down(B * HALVES - 1)


_INS = ["x", "ctx_1024", "mask_1x1xSxS2_bk0", "mask_BxSxS2_bk1", "g_xattn", "g_ffn", "L0_xattn_Wq", "L0_xattn_bq",
        "L0_xattn_Wk", "L0_xattn_bk", "L0_xattn_Wv", "L0_xattn_bv", "L0_xattn_Wo", "L0_xattn_bo", "L0_ffn_weight",
        "L1_xattn_W_Q", "L1_xattn_b_Q", "L1_xattn_W_K", "L1_xattn_b_K", "L1_xattn_W_V", "L1_xattn_b_V",
        "L1_xattn_W_out", "L1_xattn_b_out", "L1_ffn_Wg", "L1_ffn_W1", "L1_ffn_W2", "L1_ffn_W3", "L1_ffn_Ws1",
        "L1_ffn_Ws2", "L1_ffn_Ws3"]


def kernel(**inputs):
    import numpy as _np
    import concourse.bacc as _bacc
    from concourse import mybir as _mybir
    from concourse.bass_utils import run_bass_kernel_spmd as _run

    nc = _bacc.Bacc("TRN2", target_bir_lowering=False, num_devices=1)
    arrays, args = {}, {}

    def give(name, array):
        arrays[f"in_{name}"] = array
        args[name] = nc.dram_tensor(f"in_{name}", array.shape, _mybir.dt.from_np(array.dtype), kind="ExternalInput").ap()

    for name in _INS:
        give(name, _np.ascontiguousarray(inputs[name]))
    had = _np.array([[1.0]])
    while had.shape[0] < 128:
        had = _np.block([[had, had], [had, -had]])
    give("hadamard", (had / _np.sqrt(128)).astype(_np.float32))
    out = nc.dram_tensor("out_0", (2, 256, 128), _mybir.dt.float32, kind="ExternalOutput").ap()
    build(nc, args, out)
    r = _run(nc, [arrays], core_ids=[0])
    return r.results[0]["out_0"]
```
